# Optimizing a Trainium2 kernel written in Bass

```python
import numpy as np
import jax
import jax.numpy as jnp

def _softmax(x, axis=-1):
    return jax.nn.softmax(x, axis=axis)

def _gelu(x):
    return jax.nn.gelu(x, approximate=True)

def _silu(x):
    return jax.nn.silu(x)

def _sigmoid(x):
    return jax.nn.sigmoid(x)

def _layernorm(x, axis=-1, eps=1e-05):
    m = jnp.mean(x, axis=axis, keepdims=True)
    v = jnp.var(x, axis=axis, keepdims=True)
    return (x - m) / jnp.sqrt(v + eps)

def _scatter_add(tgt, idx, src, axis=0):
    return tgt.at[idx].add(src)

def _segment_sum(src, seg, n):
    return jax.ops.segment_sum(src, seg, n)
kernel_name = 'mk_decoder_preln_d1_seqx_r8_586054'

def setup_inputs(seed: int=0):
    np.random.seed(seed)
    _w = jnp.asarray

    def _rec_inputs():
        import jax
        import jax.numpy as jnp
        _rk = jax.random.key(seed)
        x = -0.0002928 + 1 * jax.random.normal(jax.random.fold_in(_rk, 1), (1, 1024, 128), jnp.float32)
        _lenS = 1024 - jax.random.randint(jax.random.fold_in(_rk, 7), (1,), 0, max(1, 1024 // 4) + 1, jnp.int32)
        _lenS2 = 6404 - jax.random.randint(jax.random.fold_in(_rk, 8), (1,), 0, max(1, 6404 // 4) + 1, jnp.int32)
        _ctx_1024P = jax.random.normal(jax.random.fold_in(_rk, 11), (1, 16, 128), jnp.float32)
        _ctx_1024c = jax.random.dirichlet(jax.random.fold_in(_rk, 511), 0.3 * jnp.ones((16,), jnp.float32), (1, 6404))
        _ctx_1024t = jnp.einsum('bsk,bkd->bsd', _ctx_1024c, _ctx_1024P)
        _ctx_1024t = _ctx_1024t * jax.lax.rsqrt(jnp.mean(jnp.square(_ctx_1024t)) + 1e-12) * 0.953939
        ctx_1024 = -1.39393e-06 + 0.999914 * (_ctx_1024t + 0.3 * jax.random.normal(jax.random.fold_in(_rk, 611), (1, 6404, 128), jnp.float32))
        return (x, ctx_1024)
    x, ctx_1024 = _rec_inputs()

    def _L0_attn_setup():
        import math
        import jax, jax.numpy as jnp
        import numpy as np
        D_MODEL = 128
        N_HEADS = 16
        D_K = D_MODEL // N_HEADS
        D_C = 32
        B, S = (2, 256)
        key = jax.random.key(seed)
        ks = jax.random.split(key, 7)
        sd = lambda fan_in: 1.0 / math.sqrt(fan_in)
        return {'x': jax.random.normal(ks[0], (B, S, D_MODEL), dtype=jnp.float32), 'W_dq': jax.random.uniform(ks[1], (D_MODEL, D_C), minval=-sd(D_MODEL), maxval=sd(D_MODEL), dtype=jnp.float32), 'W_uq': jax.random.uniform(ks[2], (D_C, N_HEADS * D_K), minval=-sd(D_C), maxval=sd(D_C), dtype=jnp.float32), 'W_dkv': jax.random.uniform(ks[3], (D_MODEL, D_C), minval=-sd(D_MODEL), maxval=sd(D_MODEL), dtype=jnp.float32), 'W_uk': jax.random.uniform(ks[4], (D_C, N_HEADS * D_K), minval=-sd(D_C), maxval=sd(D_C), dtype=jnp.float32), 'W_uv': jax.random.uniform(ks[5], (D_C, N_HEADS * D_K), minval=-sd(D_C), maxval=sd(D_C), dtype=jnp.float32), 'W_o': jax.random.uniform(ks[6], (N_HEADS * D_K, D_MODEL), minval=-sd(N_HEADS * D_K), maxval=sd(N_HEADS * D_K), dtype=jnp.float32)}
    _L0_attn_all = _L0_attn_setup()
    _L0_attn_in = {k: v for k, v in _L0_attn_all.items() if k in ('W_dq', 'W_uq', 'W_dkv', 'W_uk', 'W_uv', 'W_o')}
    del _L0_attn_all

    def _L0_xattn_setup():
        import jax, jax.numpy as jnp
        import numpy as np
        B, L, D = (2, 256, 128)
        N, H = (16, D // 16)
        key = jax.random.key(seed)
        ks = jax.random.split(key, 7)
        q_in = jax.random.normal(ks[0], (B, L, D), dtype=jnp.float32)
        k_in = jax.random.normal(ks[1], (B, L, D), dtype=jnp.float32)
        v_in = jax.random.normal(ks[2], (B, L, D), dtype=jnp.float32)
        lim_in = np.sqrt(6.0 / (D + D))
        Wq = jax.random.uniform(ks[3], (D, N, H), jnp.float32, -lim_in, lim_in)
        Wk = jax.random.uniform(ks[4], (D, N, H), jnp.float32, -lim_in, lim_in)
        Wv = jax.random.uniform(ks[5], (D, N, H), jnp.float32, -lim_in, lim_in)
        Wo = jax.random.uniform(ks[6], (N, H, D), jnp.float32, -lim_in, lim_in)
        return {'query_input': q_in, 'key_input': k_in, 'value_input': v_in, 'Wq': Wq, 'Wk': Wk, 'Wv': Wv, 'Wo': Wo}
    _L0_xattn_all = _L0_xattn_setup()
    _L0_xattn_in = {k: v for k, v in _L0_xattn_all.items() if k in ('Wq', 'Wk', 'Wv', 'Wo')}
    del _L0_xattn_all

    def _L0_ffn_setup():
        import jax, jax.numpy as jnp
        import numpy as np
        BLOCK = 32
        W_BITS = 4
        ACT_BITS = 16

        def act_qdq(x):
            qmax = 2.0 ** (ACT_BITS - 1) - 1.0
            scale = jnp.maximum(jnp.max(jnp.abs(x)) / qmax, 1e-12)
            return jnp.clip(jnp.round(x / scale), -qmax - 1.0, qmax) * scale

        def fixed_qdq_u16(x):
            scale = 1.0 / 65536.0
            return jnp.clip(jnp.round(x / scale), 0.0, 65535.0) * scale

        def lpbq_dequant(w):
            O, I = w.shape
            qmax = 2.0 ** (W_BITS - 1) - 1.0
            wb = w.reshape(O, I // BLOCK, BLOCK)
            s = jnp.maximum(jnp.max(jnp.abs(wb), axis=-1, keepdims=True) / qmax, 1e-12)
            wq = jnp.clip(jnp.round(wb / s), -qmax - 1.0, qmax) * s
            return wq.reshape(O, I)
        key = jax.random.key(seed)
        k1, k2, k3, k4 = jax.random.split(key, 4)
        B, S, H, I = (2, 512, 128, 384)
        x = jax.random.normal(k1, (B, S, H), jnp.float32)
        w_gate = jax.random.normal(k2, (I, H), jnp.float32) * 0.02
        w_up = jax.random.normal(k3, (I, H), jnp.float32) * 0.02
        w_down = jax.random.normal(k4, (H, I), jnp.float32) * 0.02
        return {'x': x, 'w_gate': w_gate, 'w_up': w_up, 'w_down': w_down}
    _L0_ffn_all = _L0_ffn_setup()
    _L0_ffn_in = {k: v for k, v in _L0_ffn_all.items() if k in ('w_gate', 'w_up', 'w_down')}
    del _L0_ffn_all
    return {'x': x, 'ctx_1024': ctx_1024, 'L0_attn_W_dq': _L0_attn_in['W_dq'], 'L0_attn_W_uq': _L0_attn_in['W_uq'], 'L0_attn_W_dkv': _L0_attn_in['W_dkv'], 'L0_attn_W_uk': _L0_attn_in['W_uk'], 'L0_attn_W_uv': _L0_attn_in['W_uv'], 'L0_attn_W_o': _L0_attn_in['W_o'], 'L0_xattn_Wq': _L0_xattn_in['Wq'], 'L0_xattn_Wk': _L0_xattn_in['Wk'], 'L0_xattn_Wv': _L0_xattn_in['Wv'], 'L0_xattn_Wo': _L0_xattn_in['Wo'], 'L0_ffn_w_gate': _L0_ffn_in['w_gate'], 'L0_ffn_w_up': _L0_ffn_in['w_up'], 'L0_ffn_w_down': _L0_ffn_in['w_down']}

def reference(x, ctx_1024, L0_attn_W_dq, L0_attn_W_uq, L0_attn_W_dkv, L0_attn_W_uk, L0_attn_W_uv, L0_attn_W_o, L0_xattn_Wq, L0_xattn_Wk, L0_xattn_Wv, L0_xattn_Wo, L0_ffn_w_gate, L0_ffn_w_up, L0_ffn_w_down):
    import jax
    import jax.numpy as jnp

    def _L0_attn_ref(x, W_dq, W_uq, W_dkv, W_uk, W_uv, W_o):
        import math
        import jax, jax.numpy as jnp
        import numpy as np
        D_MODEL = 128
        N_HEADS = 16
        D_K = D_MODEL // N_HEADS
        D_C = 32
        B, S = (2, 256)
        Bx, Sx, _ = x.shape
        c_q = x @ W_dq
        Q = (c_q @ W_uq).reshape(Bx, Sx, N_HEADS, D_K)
        c_kv = x @ W_dkv
        K = (c_kv @ W_uk).reshape(Bx, Sx, N_HEADS, D_K)
        V = (c_kv @ W_uv).reshape(Bx, Sx, N_HEADS, D_K)
        scores = jnp.einsum('bqhd,bkhd->bhqk', Q, K) / math.sqrt(D_K)
        causal = jnp.tril(jnp.ones((Sx, Sx), dtype=bool))
        scores = jnp.where(causal, scores, -jnp.inf)
        attn = jax.nn.softmax(scores, axis=-1)
        out = jnp.einsum('bhqk,bkhd->bqhd', attn, V).reshape(Bx, Sx, N_HEADS * D_K)
        return out @ W_o

    def _L0_xattn_ref(query_input, key_input, value_input, Wq, Wk, Wv, Wo):
        import jax, jax.numpy as jnp
        import numpy as np
        B, L, D = (2, 256, 128)
        N, H = (16, D // 16)
        q = jnp.einsum('bfd,dnh->bfnh', query_input, Wq)
        k = jnp.einsum('btd,dnh->btnh', key_input, Wk)
        v = jnp.einsum('btd,dnh->btnh', value_input, Wv)
        depth = Wq.shape[-1]
        q = q * depth ** (-0.5)
        logits = jnp.einsum('btnh,bfnh->bnft', k, q)
        weights = jax.nn.softmax(logits, axis=-1)
        attn = jnp.einsum('bnft,btnh->bfnh', weights, v)
        out = jnp.einsum('bfnh,nhd->bfd', attn, Wo)
        return out

    def _L0_ffn_ref(x, w_gate, w_up, w_down):
        import jax, jax.numpy as jnp
        import numpy as np
        BLOCK = 32
        W_BITS = 4
        ACT_BITS = 16

        def act_qdq(x):
            qmax = 2.0 ** (ACT_BITS - 1) - 1.0
            scale = jnp.maximum(jnp.max(jnp.abs(x)) / qmax, 1e-12)
            return jnp.clip(jnp.round(x / scale), -qmax - 1.0, qmax) * scale

        def fixed_qdq_u16(x):
            scale = 1.0 / 65536.0
            return jnp.clip(jnp.round(x / scale), 0.0, 65535.0) * scale

        def lpbq_dequant(w):
            O, I = w.shape
            qmax = 2.0 ** (W_BITS - 1) - 1.0
            wb = w.reshape(O, I // BLOCK, BLOCK)
            s = jnp.maximum(jnp.max(jnp.abs(wb), axis=-1, keepdims=True) / qmax, 1e-12)
            wq = jnp.clip(jnp.round(wb / s), -qmax - 1.0, qmax) * s
            return wq.reshape(O, I)
        x = act_qdq(x)
        up = act_qdq(x @ lpbq_dequant(w_up).T)
        gate = act_qdq(x @ lpbq_dequant(w_gate).T)
        sig = fixed_qdq_u16(jax.nn.sigmoid(gate))
        gate = act_qdq(gate * sig)
        o = act_qdq(gate * up)
        return o @ lpbq_dequant(w_down).T
    x = x + _L0_attn_ref(_layernorm(x, axis=-1), L0_attn_W_dq, L0_attn_W_uq, L0_attn_W_dkv, L0_attn_W_uk, L0_attn_W_uv, L0_attn_W_o)
    x = x + _L0_xattn_ref(_layernorm(x, axis=-1), ctx_1024, ctx_1024, L0_xattn_Wq, L0_xattn_Wk, L0_xattn_Wv, L0_xattn_Wo)
    x = x + _L0_ffn_ref(_layernorm(x, axis=-1), L0_ffn_w_gate, L0_ffn_w_up, L0_ffn_w_down)
    return x

_drawn_inputs = setup_inputs


def setup_inputs(seed=0):
    import zlib

    import numpy as np

    out = dict(_drawn_inputs(seed))
    spreads = {}
    factors = {'L0_attn_W_dq': 8.0,
     'L0_attn_W_uq': 8.0,
     'L0_attn_W_dkv': 3.847,
     'L0_attn_W_uk': 8.0,
     'L0_attn_W_uv': 3.416,
     'L0_attn_W_o': 3.411,
     'L0_ffn_w_gate': 5.748,
     'L0_ffn_w_up': 5.315,
     'L0_ffn_w_down': 5.405}
    for name, (base, spread) in spreads.items():
        noise = np.random.default_rng([zlib.crc32(name.encode()), seed]).standard_normal(out[name].shape)
        drawn = base * np.exp(spread * noise) if base else spread * noise
        out[name] = jnp.asarray(drawn.astype(out[name].dtype))
    for name, factor in factors.items():
        out[name] = (out[name] * factor).astype(out[name].dtype)
    return out
```

```python
from contextlib import ExitStack

import numpy as np

import concourse.bass as bass
from concourse import mybir

S, SC, D, H, DK, DC, FF = 1024, 6404, 128, 16, 8, 32, 384
P = 128
NT = S // P
NP = H // 2
KT = SC // P + 1
TAIL = SC - (KT - 1) * P
CH = 4
NCH = KT // CH
REST = SC - NCH * CH * P
KPART = (0, 0, 0, 1, 1, 2)
QPART = (0, 1, 2, 0, 1, 0)
TERMS = len(KPART)
CONST_ROW, ROWS = 96, 100
BLK = 32
QMAX, WMAX = 32767.0, 7.0
MAGIC = 1.5 * 2.0 ** 23
MASKED = -1.0e38
SAFE = 40.0
EPS = 1e-5


def build(nc, x, ctx, wdq, wuq, wdkv, wuk, wuv, wo_s, wq, wk, wv, wo_x, wg, wu, wd,
          ident_in, mask_in, heads_in, out, force_exact=False, stop=9):
    f32, bf16, i32 = mybir.dt.float32, mybir.dt.bfloat16, mybir.dt.int32
    ALU, ACT, AX = mybir.AluOpType, mybir.ActivationFunctionType, mybir.AxisListType
    ABSMAX = bass.bass_isa.ReduceOp.absmax

    st = ExitStack()
    with st:
        def sb(name, shape, dt=f32):
            return st.enter_context(nc.sbuf_tensor(name, shape, dt))

        def sem(name):
            return st.enter_context(nc.semaphore(name))

        q_dram = nc.dram_tensor("q_parts", (2, 3, P, S), bf16, kind="Internal").ap()
        ks_dram = nc.dram_tensor("self_k_parts", (3, P, S), bf16, kind="Internal").ap()
        kx_dram = nc.dram_tensor("ctx_k_parts", (3, P, KT * P), bf16, kind="Internal").ap()

        ident = sb("ident", [P, P])
        identb = sb("identb", [P, P], bf16)
        mask = sb("mask", [P, 2, P], bf16)
        headsum = sb("headsum", [P, P], bf16)
        zeros = sb("zeros", [P, P], bf16)
        eps = sb("eps", [P, 1])
        w_dq = sb("w_dq", [D, DC])
        w_uq = sb("w_uq", [DC, D])
        w_dkv = sb("w_dkv", [D, DC])
        w_uk = sb("w_uk", [DC, D])
        w_uv = sb("w_uv", [DC, D])
        w_os = sb("w_os", [D, D])
        w_q = sb("w_q", [D, D])
        w_k = sb("w_k", [D, D])
        w_v = sb("w_v", [D, D])
        w_ox = sb("w_ox", [D, D])
        wraw = sb("wraw", [P, 9, P])
        wmax = sb("wmax", [P, 36])
        wscale = sb("wscale", [P, 36])
        wT = sb("wT", [P, 9, P])

        X = sb("X", [P, NT, D])
        XN = sb("XN", [P, NT, D])
        XT = sb("XT", [D, S])
        stats = sb("stats", [P, NT, 6])
        moments = sb("moments", [P, NT, 2])
        std = sb("std", [P, NT])
        rstd = sb("rstd", [P, NT])
        part = sb("part", [P, 3, S], bf16)
        kpart = sb("kpart", [P, 3, S], bf16)
        QQ = sb("QQ", [P, H, S], bf16)
        KS = sb("KS", [ROWS, NP, S], bf16)
        KX = sb("KX", [ROWS, 2, NP, P], bf16)
        VS = sb("VS", [P, NT, 4, 4, 32])
        V9 = sb("V9", [P, KT, H, 9])
        VX = sb("VX", [P, 2, 4, 4, 32])
        PR = sb("PR", [P, 8, S])
        OT = sb("OT", [P, 2, S])
        rec = sb("rec", [P, 4, NT, 4])
        mx = sb("mx", [P, H * NT])
        mtmp = sb("mtmp", [P, NT])
        npart = sb("npart", [P, 3, H * NT], bf16)
        nrem = sb("nrem", [P, H * NT])
        nT = sb("nT", [P, 3, P], bf16)
        C = sb("C", [P, 2, CH, D])
        CT = sb("CT", [D, 2, CH * P])
        cpart = sb("cpart", [P, 2, 3, CH * P], bf16)
        crem = sb("crem", [P, CH * P])
        csq = sb("csq", [P, 2, CH * P], bf16)
        kn = sb("kn", [P, NCH + 1])
        col = sb("col", [P, 24])
        flag = sb("flag", [1, 1], i32)
        ps = st.enter_context(nc.psum_tensor("ps", [P, 8, 512], f32))

        lat = PR[0:DC, 0:2, :]
        rem, qf = OT[:, 0, :], OT[:, 1, :]
        UP = PR[:, 0:3, :]
        GA = PR[:, 3:6, :]
        FB = QQ[:, 0:6, :].bitcast(f32).rearrange("p (t a) s -> p t (a s)", t=3)

        wb = wraw[:].rearrange("p t (b i) -> p (t b) i", i=BLK)
        sc, winv = (w[:].rearrange("p (b o) -> p b o", o=1).to_broadcast([P, 36, BLK]) for w in (wscale, wmax))

        names = """consts x_loaded weights_loaded ffn_w_loaded ctx_tail_loaded ctx_t_ready ctxT_ready k_ready k_split
            v_ready v_copied k_parts sq_ready n_ready pool_step dve_step kx_tail_stored q_stored q_spread ks_stored
            ks_spread out_stored w_t_ready w_t_copied flag_ready exact_rows bound_col bound_all bound_sd
            lat_ready lat_copied qk_ready qk_copied vs_ready vs_copied m_scores m_reduced neg_parts neg_t neg_copied
            neg_rows self_ready self_exp self_pv xs_ready x_exp x_pv x_ktile v_staged v_freed xq_ready xq_parts xsq x_norm
            xq_stored xq_spread slow_loaded slow_scores slow_reduced slow_neg slow_t slow_copied slow_rows
            rows_ready kconst am_col am_all up_ready up_copied gate_ready gate_copied sig_done oq_ready oqT_ready oqT_copied
            y_ready pool_init prep_credit x_scaled identb_ready w_ready""".split()
        s = {n: sem(n) for n in names}
        ctx_loaded = [sem(f"ctx_loaded{b}") for b in range(2)]
        k_stored = [sem(f"k_stored{b}") for b in range(2)]
        kx_loaded = [sem(f"kx_loaded{b}") for b in range(2)]
        ln = [{n: sem(f"ln{k}_{n}") for n in ("var", "std", "norm", "T", "copied")} for k in range(3)]
        fin = [{n: sem(f"fin{k}_{n}") for n in ("oT", "attn", "back", "attnT", "attnTc", "y", "res")} for k in range(2)]

        CREDIT = 2
        credited = ("ctx_t_ready", "ctxT_ready", "k_ready", "k_split", "v_ready", "v_copied", "k_parts",
                    "sq_ready", "n_ready")

        def fill_rows(eng, dst, src, terms, done):
            for i, part_no in enumerate(terms):
                eng.dma_start(dst[i * 16:i * 16 + 16], src[part_no].rearrange("(p r) n -> r p n", r=16)).then_inc(done, 16)

        def fill_queries(eng, k, done):
            for i, part_no in enumerate(QPART):
                for slot in range(2):
                    r = i * 16 + slot * 8
                    eng.dma_start(QQ[r:r + 8, slot:H:2, :],
                                  q_dram[k, part_no].rearrange("(p s d) n -> s d p n", s=2, d=DK)[slot]).then_inc(done, 16)

        def neg_fill(eng, done):
            for i in range(3):
                eng.dma_start(QQ[97 + i:98 + i, :, :].rearrange("o h (t q) -> o (h t) q", q=P),
                              nT[:, i, :]).then_inc(done, 16)

        block = st.enter_context(nc.Block())

        @block.sync
        def _(sp):
            sp.dma_start(ident[:], ident_in).then_inc(s["consts"], 16)
            for dst, src in ((w_k, wk), (w_v, wv)):
                sp.dma_start(dst[:], src.rearrange("d n h -> d (n h)")).then_inc(s["consts"], 16)
            sp.dma_start(headsum[:], heads_in).then_inc(s["consts"], 16)
            sp.dma_start(X[:], x[0].rearrange("(t p) d -> p t d", p=P)).then_inc(s["x_loaded"], 16)
            sp.dma_start(mask[:], mask_in).then_inc(s["weights_loaded"], 16)
            sp.dma_start(w_q[:], wq.rearrange("d n h -> d (n h)")).then_inc(s["weights_loaded"], 16)
            sp.dma_start(w_ox[:], wo_x.rearrange("n h d -> (n h) d")).then_inc(s["weights_loaded"], 16)
            for dst, src in ((w_dq, wdq), (w_uq, wuq), (w_dkv, wdkv), (w_uk, wuk), (w_uv, wuv), (w_os, wo_s)):
                sp.dma_start(dst[:], src).then_inc(s["weights_loaded"], 16)
            for k, w in enumerate((wg, wu)):
                sp.dma_start(wraw[:, 3 * k:3 * k + 3, :], w.rearrange("(t p) i -> p t i", p=P)).then_inc(s["ffn_w_loaded"], 16)
            sp.dma_start(wraw[:, 6:9, :], wd.rearrange("o (t i) -> o t i", i=P)).then_inc(s["ffn_w_loaded"], 16)
            sp.wait_ge(s["prep_credit"], len(credited))
            cv = ctx[0, 0:NCH * CH * P, :].rearrange("(c t p) d -> c p t d", p=P, t=CH)
            with sp.Fori(0, NCH // 2) as i:
                for b in range(2):
                    sp.wait_ge(s["ctx_t_ready"], 2 * i + (b + 1))
                    sp.dma_start(C[:, b, :, :], cv[bass.ds(2 * i + b, 1)].rearrange("c p t d -> p (c t) d")).then_inc(ctx_loaded[b], 16)
            sp.wait_ge(s["ctx_t_ready"], NCH + 1)
            lo = NCH * CH * P
            sp.dma_start(C[:, 0, 0:2, :], ctx[0, lo:lo + 2 * P, :].rearrange("(t p) d -> p t d", p=P)).then_inc(s["ctx_tail_loaded"], 16)
            sp.dma_start(C[0:TAIL, 0, 2, :], ctx[0, lo + 2 * P:SC, :]).then_inc(s["ctx_tail_loaded"], 16)

            sp.wait_ge(s["qk_copied"], 2)
            sp.dma_start(q_dram[0].rearrange("i p n -> p i n"), part[:]).then_inc(s["q_stored"], 16)
            sp.dma_start(ks_dram.rearrange("i p n -> p i n"), kpart[:]).then_inc(s["ks_stored"], 16)
            sp.wait_ge(s["pool_init"], 1)
            sp.wait_ge(s["q_stored"], 16)
            fill_queries(sp, 0, s["q_spread"])
            sp.wait_ge(s["ks_stored"], 16)
            fill_rows(sp, KS[:], ks_dram, KPART, s["ks_spread"])
            sp.wait_ge(s["neg_copied"], 1)
            neg_fill(sp, s["neg_rows"])
            if stop == 1:
                sp.wait_ge(fin[0]["res"], 1)
                sp.dma_start(out[0].rearrange("(t p) d -> p t d", p=P), X[:]).then_inc(s["out_stored"], 16)
                sp.wait_ge(s["out_stored"], 16)
                return

            sp.wait_ge(s["xq_parts"], 1)
            sp.dma_start(q_dram[1].rearrange("i p n -> p i n"), part[:]).then_inc(s["xq_stored"], 16)
            sp.wait_ge(s["xq_stored"], 16)
            fill_queries(sp, 1, s["xq_spread"])
            sp.wait_ge(k_stored[0], 16 * (NCH // 2))
            sp.wait_ge(k_stored[1], 16 * (NCH // 2))
            sp.wait_ge(s["kx_tail_stored"], 16)

            def load_keys(t, n, b, done):
                for i, part_no in enumerate(KPART):
                    src = kx_dram[part_no, :, bass.ds(t * P, n)]
                    sp.dma_start(KX[i * 16:i * 16 + 16, b, :, 0:n], src.rearrange("(p r) n -> r p n", r=16)).then_inc(done, 16)

            sp.wait_ge(s["flag_ready"], 1)
            exact = sp.value_load(flag[0:1, 0:1], min_val=0, max_val=1)
            with sp.If(exact > 0):
                load_keys(0, P, 0, s["slow_loaded"])
                with sp.Fori(1, KT - 1) as t:
                    sp.wait_ge(s["slow_scores"], t * H)
                    load_keys(t, P, 0, s["slow_loaded"])
                sp.wait_ge(s["slow_scores"], (KT - 1) * H)
                load_keys(KT - 1, TAIL, 0, s["slow_loaded"])
                sp.wait_ge(s["slow_copied"], 1)
                neg_fill(sp, s["slow_rows"])
            load_keys(0, P, 0, kx_loaded[0])
            with sp.Fori(0, (KT - 3) // 2) as i:
                for k in range(2):
                    sp.wait_ge(s["xs_ready"], i * (2 * H) + (k * H + 1))
                    load_keys(2 * i + (1 + k), P, (1 + k) % 2, kx_loaded[(1 + k) % 2])
            sp.wait_ge(s["xs_ready"], (KT - 3) * H)
            load_keys(KT - 2, P, (KT - 2) % 2, kx_loaded[(KT - 2) % 2])
            sp.wait_ge(s["xs_ready"], (KT - 2) * H)
            load_keys(KT - 1, TAIL, (KT - 1) % 2, kx_loaded[(KT - 1) % 2])
            if stop == 2:
                sp.wait_ge(fin[1]["res"], 1)
                sp.dma_start(out[0].rearrange("(t p) d -> p t d", p=P), X[:]).then_inc(s["out_stored"], 16)
                sp.wait_ge(s["out_stored"], 16)
                return
            ov = out[0].rearrange("(t p) d -> p t d", p=P)
            for half in range(2):
                sp.wait_ge(s["x_scaled"], half + 1)
                sp.dma_start(ov[:, 4 * half:4 * half + 4, :], XN[:, 4 * half:4 * half + 4, :]).then_inc(s["out_stored"], 16)
            sp.wait_ge(s["out_stored"], 32)

        @block.gpsimd
        def _(pool):
            for n in credited:
                pool.memset(eps[:], EPS).then_inc(s[n], CREDIT)
                pool.wait_ge(s[n], CREDIT)
                pool.memset(col[:, 0:1], 0.0).then_inc(s["prep_credit"], 1)
                pool.wait_ge(s["prep_credit"], 1 + credited.index(n))
            steps = [0]

            def step(ins):
                steps[0] += 1
                ins.then_inc(s["pool_step"], 1)
                pool.wait_ge(s["pool_step"], steps[0])

            pool.memset(zeros[:], 0.0).then_inc(s["m_reduced"], 4)
            step(pool.memset(V9[:, 0:KT - 1, :, 8:9], 1.0))
            step(pool.memset(V9[:, KT - 1, :, :], 0.0))
            step(pool.memset(V9[0:TAIL, KT - 1, :, 8:9], 1.0))
            step(pool.memset(VX[:], 0.0))
            step(pool.memset(VS[:], 0.0))
            step(pool.memset(VS[:, :, :, :, 8:9], 1.0))
            step(pool.memset(KS[96:ROWS], 1.0))
            step(pool.memset(KS[96:97], 0.0))
            step(pool.memset(KX[96:ROWS], 1.0))
            step(pool.memset(QQ[0:96, :, :].bitcast(i32), 0))
            step(pool.memset(QQ[96:ROWS, :, :], 0.0))
            pool.memset(QQ[96:97, :, :], 1.0).then_inc(s["pool_init"], 1)

            kv = kx_dram.rearrange("i p n -> p i n")
            with pool.Fori(0, NCH // 2) as i:
                for b in range(2):
                    pool.wait_ge(s["k_parts"], 2 * i + (b + 1 + CREDIT))
                    pool.dma_start(kv[:, :, bass.ds((2 * i + b) * (CH * P), CH * P)], cpart[:, b, :, :]).then_inc(k_stored[b], 16)
            pool.wait_ge(s["k_parts"], NCH + 1 + CREDIT)
            pool.dma_start(kv[:, :, NCH * CH * P:SC], cpart[:, 0, :, 0:REST]).then_inc(s["kx_tail_stored"], 16)
            if stop == 1:
                pool.wait_ge(s["kx_tail_stored"], 16)
                return
            pool.wait_ge(s["bound_col"], 1)
            pool.partition_all_reduce(col[:, 2:3], col[:, 1:2], P, ABSMAX).then_inc(s["bound_all"], 1)
            if stop == 2:
                return
            for k in range(5):
                pool.wait_ge(s["am_col"], k + 1)
                pool.partition_all_reduce(col[:, 9:10], col[:, 8:9], P, ABSMAX).then_inc(s["am_all"], 1)

        @block.scalar
        def _(act):
            asteps = [0]

            def copy_ctx(c, b, n):
                act.wait_ge(s["ctx_t_ready"], c + (1 + CREDIT))
                act.wait_ge(s["v_ready"], c + 1)
                act.activation(CT[:, b, 0:n], ps[:, b, 0:n], ACT.Copy).then_inc(s["ctxT_ready"], 1)

            def copy_v(c, b, dst, src):
                act.wait_ge(s["v_ready"], c + (1 + CREDIT))
                return act.activation(dst, src, ACT.Copy)

            act.wait_ge(s["prep_credit"], len(credited))
            act.wait_ge(s["pool_step"], 3)
            with act.Fori(0, NCH // 2) as i:
                for b in range(2):
                    copy_ctx(2 * i + b, b, CH * P)
                    copy_v(2 * i + b, b, V9[:, bass.ds((2 * i + b) * CH, CH), :, 0:8],
                           ps[:, 4 + b, :].rearrange("p (t h d) -> p t h d", t=CH, d=DK)).then_inc(s["v_copied"], 1)
            copy_ctx(NCH, 0, REST)
            last = copy_v(NCH, 0, V9[:, NCH * CH:NCH * CH + 2, :, 0:8],
                          ps[:, 4, 0:2 * P].rearrange("p (t h d) -> p t h d", t=2, d=DK))
            act.activation(V9[0:TAIL, KT - 1, :, 0:8], ps[0:TAIL, 4, 2 * P:3 * P].rearrange("p (h d) -> p h d", d=DK),
                           ACT.Copy).then_inc(s["v_copied"], 1)
            for g in range(3):
                act.wait_ge(s["w_t_ready"], g + 1)
                act.activation(wT[:, 3 * g:3 * g + 3, :], ps[:, 5 + g, 0:3 * P].rearrange("p (t i) -> p t i", i=P),
                               ACT.Copy).then_inc(s["w_t_copied"], 1)

            def norm(k):
                act.wait_ge(ln[k]["var"], 1)
                act.activation(std[:], moments[:, :, 1:2].rearrange("p t o -> p (t o)"), ACT.Sqrt, bias=eps[:]).then_inc(ln[k]["std"], 1)
                for half in range(2):
                    act.wait_ge(ln[k]["T"], half + 1)
                    act.activation(XT[:, half * 512:half * 512 + 512], ps[:, half, :], ACT.Copy).then_inc(ln[k]["copied"], 1)

            norm(0)
            for half in range(2):
                act.wait_ge(s["lat_ready"], 2 * half + 2)
                act.activation(lat[:, 1, half * 512:half * 512 + 512], ps[0:DC, 4 + half, :], ACT.Copy).then_inc(s["lat_copied"], 1)
            act.wait_ge(s["pool_step"], 6)
            for t in range(NT):
                act.wait_ge(s["vs_ready"], t // 4 + 1)
                act.activation(VS[:, t, :, :, 0:8],
                               ps[:, 6 + t // 4, (t % 4) * P:(t % 4) * P + P].rearrange("p (j c d) -> p c j d", j=4, d=DK),
                               ACT.Copy).then_inc(s["vs_copied"], 1)

            for u in range(NT * H):
                kt = u // H
                act.wait_ge(s["self_ready"], u + 1)
                if u % 4 == 0 and u >= 8:
                    act.wait_ge(s["self_pv"], u // 4 - 1)
                act.activation(PR[:, u % 8, kt * P:S],
                               ps[:, 2 * (u % 2):2 * (u % 2) + 2, :].rearrange("p b n -> p (b n)")[:, kt * P:S],
                               ACT.Exp).then_inc(s["self_exp"], 1)

            def finish(k, pv, groups):
                act.wait_ge(pv, groups)
                act.activation(OT[:, 1, :], ps[:, 6:8, :].rearrange("p b n -> p (b n)"), ACT.Copy).then_inc(fin[k]["oT"], 1)
                act.wait_ge(fin[k]["attnT"], 1)
                act.activation(XT[:, 0:512], ps[:, 0, :], ACT.Copy).then_inc(fin[k]["attnTc"], 1)
                act.wait_ge(fin[k]["attnT"], 2)
                act.activation(XT[:, 512:S], ps[:, 1, :], ACT.Copy).then_inc(fin[k]["attnTc"], 1)

            finish(0, s["self_pv"], NT * H // 4)
            if stop == 1:
                return
            norm(1)
            act.wait_ge(s["bound_all"], 1)
            act.activation(col[:, 3:4], col[:, 2:3], ACT.Sqrt).then_inc(s["bound_sd"], 1)

            def exp_tile(t):
                for h in range(H):
                    act.wait_ge(s["xs_ready"], t * H + (h + 1))
                    if h % 4 == 0 and not (isinstance(t, int) and t * 4 + h // 4 < 2):
                        act.wait_ge(s["x_pv"], t * 4 + (h // 4 - 1))
                    act.activation(PR[:, h % 8, :], ps[:, 2 * (h % 2):2 * (h % 2) + 2, :].rearrange("p b n -> p (b n)"),
                                   ACT.Exp).then_inc(s["x_exp"], 1)

            exp_tile(0)
            with act.Fori(0, (KT - 3) // 2) as i:
                exp_tile(2 * i + 1)
                exp_tile(2 * i + 2)
            exp_tile(KT - 2)
            exp_tile(KT - 1)
            finish(1, s["x_pv"], KT * H // 4)
            if stop == 2:
                return
            norm(2)
            for t in range(3):
                act.wait_ge(s["up_ready"], t + 1)
                act.activation(UP[:, t, :], ps[:, 2 * (t % 4):2 * (t % 4) + 2, :].rearrange("p b n -> p (b n)"), ACT.Copy,
                               scale=col[:, 10:11]).then_inc(s["up_copied"], 1)
            act.wait_ge(s["gate_copied"], 1)
            act.activation(FB, GA, ACT.Sigmoid, scale=col[:, 14:15]).then_inc(s["sig_done"], 1)

        @block.vector
        def _(dve):
            steps = [0]

            def step(ins, off=0):
                steps[0] += 1
                ins.then_inc(s["dve_step"], 1)
                dve.wait_ge(s["dve_step"], off + steps[0])

            dve.wait_ge(s["prep_credit"], len(credited))
            dve.wait_ge(s["consts"], 64)
            dve.tensor_copy(identb[:], ident[:]).then_inc(s["identb_ready"], 1)

            PER = 2 * 3

            def split_chunk(c, b, n, off):
                dve.wait_ge(s["k_ready"], c + (1 + CREDIT))
                src = ps[:, 2 + b, 0:n]
                step(dve.tensor_copy(cpart[:, b, 0, 0:n], src), off)
                dve.tensor_tensor(crem[:, 0:n], src, cpart[:, b, 0, 0:n], ALU.subtract).then_inc(s["k_split"], 1)
                dve.wait_ge(s["k_split"], c + (1 + CREDIT))
                step(dve.tensor_copy(cpart[:, b, 1, 0:n], crem[:, 0:n]), off)
                dve.tensor_tensor(cpart[:, b, 2, 0:n], crem[:, 0:n], cpart[:, b, 1, 0:n], ALU.subtract).then_inc(s["k_parts"], 1)
                dve.tensor_tensor(csq[:, b, 0:n], cpart[:, b, 0, 0:n], cpart[:, b, 0, 0:n], ALU.mult).then_inc(s["sq_ready"], 1)
                dve.wait_ge(s["n_ready"], c + (1 + CREDIT))

            for b in range(2):
                split_chunk(b, b, CH * P, 0)
                step(dve.reduce_max(kn[:, b:b + 1], ps[:, 6 + b, :], AX.X))
            with dve.Fori(1, NCH // 2) as i:
                first = steps[0]
                for b in range(2):
                    dve.wait_ge(k_stored[b], 16 * i)
                    split_chunk(2 * i + b, b, CH * P, i * PER - PER)
                    step(dve.reduce_max(kn[:, bass.ds(2 * i + b, 1)], ps[:, 6 + b, :], AX.X), i * PER - PER)
                assert steps[0] - first == PER
            steps[0] += PER * (NCH // 2 - 2)
            dve.wait_ge(k_stored[0], 16 * (NCH // 2))
            split_chunk(NCH, 0, REST, 0)
            step(dve.reduce_max(kn[:, NCH:NCH + 1], ps[:, 6, 0:REST], AX.X))
            step(dve.reduce_max(col[:, 0:1], kn[:], AX.X))

            dve.wait_ge(s["ffn_w_loaded"], 48)
            step(dve.tensor_reduce(wmax[:], wb, AX.X, ALU.max, apply_absolute_value=True))
            step(dve.tensor_scalar(wscale[:], wmax[:], 1.0 / WMAX, 1e-12, ALU.mult, ALU.max))
            step(dve.reciprocal(wmax[:], wscale[:]))
            step(dve.tensor_tensor(wb, wb, winv, ALU.mult))
            step(dve.tensor_scalar(wraw[:], wraw[:], MAGIC, -MAGIC, ALU.add, ALU.add))
            step(dve.tensor_scalar(wraw[:], wraw[:], -WMAX - 1.0, WMAX, ALU.max, ALU.min))
            dve.tensor_tensor(wb, wb, sc, ALU.mult).then_inc(s["w_ready"], 1)

            def norm(k):
                for t in range(NT):
                    last = dve.bn_stats(stats[:, t, :], X[:, t, :])
                step(last)
                for t in range(NT):
                    last = dve.bn_aggr(moments[:, t, :], stats[:, t, :])
                last.then_inc(ln[k]["var"], 1)
                dve.wait_ge(ln[k]["std"], 1)
                step(dve.reciprocal(rstd[:], std[:]))
                for t in range(NT):
                    last = dve.tensor_scalar(XN[:, t, :], X[:, t, :], moments[:, t, 0:1], rstd[:, t:t + 1],
                                             ALU.subtract, ALU.mult)
                last.then_inc(ln[k]["norm"], 1)

            def split(dst, src, done):
                step(dve.tensor_copy(dst[:, 0, :], src))
                step(dve.tensor_tensor(rem, src, dst[:, 0, :], ALU.subtract))
                step(dve.tensor_copy(dst[:, 1, :], rem))
                dve.tensor_tensor(dst[:, 2, :], rem, dst[:, 1, :], ALU.subtract).then_inc(done, 1)

            dve.wait_ge(s["x_loaded"], 16)
            norm(0)
            for half in range(2):
                dve.wait_ge(s["lat_ready"], 2 * half + 1)
                last = dve.tensor_copy(lat[:, 0, half * 512:half * 512 + 512], ps[0:DC, 2 + half, :])
            last.then_inc(s["lat_copied"], 1)
            dve.wait_ge(s["qk_ready"], 1)
            step(dve.tensor_scalar(qf, ps[:, 0:2, :].rearrange("p b n -> p (b n)"), DK ** -0.5, None, ALU.mult))
            split(part[:], qf, s["qk_copied"])
            dve.wait_ge(s["qk_ready"], 2)
            dve.wait_ge(s["qk_copied"], 1)
            step(dve.tensor_copy(qf, ps[:, 2:4, :].rearrange("p b n -> p (b n)")))
            split(kpart[:], qf, s["qk_copied"])

            with dve.Fori(0, NP) as i:
                for v in range(2 * NT):
                    qt = v % NT
                    dve.wait_ge(s["m_scores"], i * (2 * NT) + (v + 1))
                    r = 2 * (v % 4)
                    dve.reduce_max(mx[:, bass.ds(i * (2 * NT) + v, 1)],
                                   ps[:, r:r + 2, :].rearrange("p b n -> p (b n)")[:, 0:(qt + 1) * P], AX.X).then_inc(s["m_reduced"], 1)
            dve.wait_ge(s["m_reduced"], H * NT + 4)

            def negate(done, t_ready, copied):
                step(dve.tensor_scalar(npart[:, 0, :], mx[:], -1.0, None, ALU.mult))
                step(dve.scalar_tensor_tensor(nrem[:], mx[:], -1.0, npart[:, 0, :], ALU.mult, ALU.subtract))
                step(dve.tensor_copy(npart[:, 1, :], nrem[:]))
                dve.tensor_tensor(npart[:, 2, :], nrem[:], npart[:, 1, :], ALU.subtract).then_inc(done, 1)
                dve.wait_ge(t_ready, 1)
                dve.tensor_copy(nT[:].rearrange("p i q -> p (i q)"), ps[:, 0, :].bitcast(bf16)[:, 0:3 * P]).then_inc(copied, 1)

            negate(s["neg_parts"], s["neg_t"], s["neg_copied"])

            def finish(k, pv, groups):
                dve.wait_ge(pv, groups)
                dve.tensor_copy(OT[:, 0, :], ps[:, 4:6, :].rearrange("p b n -> p (b n)")).then_inc(fin[k]["oT"], 1)
                dve.wait_ge(fin[k]["back"], 1)
                view = [ps[:, b0:b0 + 2, :].rearrange("p b (t r) -> p (b t) r", r=P).rearrange("p t (c r) -> p t c r", c=4)
                        for b0 in (0, 2)]
                place = [view[j // 3][:, :, :, 9 * (j % 3):9 * (j % 3) + 9] for j in range(4)]
                for j in range(4):
                    last = dve.reciprocal(rec[:, j, :, :], place[j][:, :, :, 8:9].rearrange("p t c o -> p t (c o)"))
                step(last)
                for j in range(4):
                    o = XN[:, :, j * 32:j * 32 + 32].rearrange("p t (c d) -> p t c d", c=4)
                    last = dve.tensor_tensor(o, place[j][:, :, :, 0:8],
                                             rec[:, j, :, :].rearrange("p t (c o) -> p t c o", o=1).to_broadcast([P, NT, 4, DK]), ALU.mult)
                last.then_inc(fin[k]["attn"], 1)
                dve.wait_ge(fin[k]["y"], 1)
                dve.tensor_tensor(X[:].rearrange("p t d -> p (t d)"), X[:].rearrange("p t d -> p (t d)"),
                                  ps[:, 2:4, :].rearrange("p b n -> p (b n)"), ALU.add).then_inc(fin[k]["res"], 1)
                dve.wait_ge(fin[k]["res"], 1)

            finish(0, s["self_pv"], NT * H // 4)
            if stop == 1:
                return
            norm(1)
            step(dve.memset(QQ[96:ROWS, :, :], 0.0))
            step(dve.memset(QQ[96:97, :, :], 1.0))
            dve.wait_ge(s["xq_ready"], 1)
            step(dve.tensor_scalar(qf, ps[:, 4:6, :].rearrange("p b n -> p (b n)"), DK ** -0.5, None, ALU.mult))
            split(part[:], qf, s["xq_parts"])
            sq = kpart[:, 0, :]
            dve.tensor_tensor(sq, part[:, 0, :], part[:, 0, :], ALU.mult).then_inc(s["xsq"], 1)
            dve.wait_ge(s["x_norm"], 1)
            step(dve.reduce_max(col[:, 4:5], ps[:, 6:8, :].rearrange("p b n -> p (b n)"), AX.X))
            dve.tensor_scalar(col[:, 1:2], col[:, 4:5], col[:, 0:1], 1.03, ALU.mult, ALU.mult).then_inc(s["bound_col"], 1)
            dve.wait_ge(s["bound_sd"], 1)
            step(dve.tensor_scalar(col[:, 4:5], col[:, 3:4], -1.0 if force_exact else SAFE, None, ALU.is_gt))
            step(dve.tensor_copy(flag[:], col[0:1, 4:5]))
            step(dve.tensor_scalar(col[:, 5:6], col[:, 4:5], -1.0, 1.0, ALU.mult, ALU.add))
            step(dve.scalar_tensor_tensor(col[:, 6:7], col[:, 3:4], -1.0, col[:, 5:6], ALU.mult, ALU.mult))
            dve.wait_ge(s["pool_init"], 1)
            dve.tensor_scalar(KX[96:97].rearrange("o b p n -> o (b p n)"), KX[96:97].rearrange("o b p n -> o (b p n)"),
                              col[96:97, 6:7], None, ALU.mult).then_inc(s["flag_ready"], 1)
            dve.wait_ge(s["flag_ready"], 1)
            exact = dve.value_load(flag[0:1, 0:1], min_val=0, max_val=1)
            with dve.If(exact > 0):
                dve.memset(mx[:], -3.0e38).then_inc(s["slow_reduced"], 4)

                def fold(t, n):
                    with dve.Fori(0, NP) as i:
                        for sl in range(2):
                            v = t * H + i * 2
                            dve.wait_ge(s["slow_scores"], v + (sl + 1))
                            dve.wait_ge(s["slow_reduced"], (v + sl) * 2 + 4)
                            dve.tensor_reduce(mtmp[:], ps[:, 2 * sl:2 * sl + 2, :].rearrange("p b (t n) -> p (b t) n", n=P)[:, :, 0:n],
                                              AX.X, ALU.max).then_inc(s["slow_reduced"], 1)
                            dve.wait_ge(s["slow_reduced"], (v + sl) * 2 + 5)
                            m = mx[:, bass.ds(i * (2 * NT) + sl * NT, NT)]
                            dve.tensor_tensor(m, m, mtmp[:], ALU.max).then_inc(s["slow_reduced"], 1)

                with dve.Fori(0, KT - 1) as t:
                    fold(t, P)
                fold(KT - 1, TAIL)
                dve.wait_ge(s["slow_reduced"], 2 * KT * H + 4)

                dve.tensor_scalar(npart[:, 0, :], mx[:], -1.0, None, ALU.mult).then_inc(s["slow_neg"], 1)
                dve.wait_ge(s["slow_neg"], 1)
                dve.scalar_tensor_tensor(nrem[:], mx[:], -1.0, npart[:, 0, :], ALU.mult, ALU.subtract).then_inc(s["slow_neg"], 1)
                dve.wait_ge(s["slow_neg"], 2)
                dve.tensor_copy(npart[:, 1, :], nrem[:]).then_inc(s["slow_neg"], 1)
                dve.wait_ge(s["slow_neg"], 3)
                dve.tensor_tensor(npart[:, 2, :], nrem[:], npart[:, 1, :], ALU.subtract).then_inc(s["slow_neg"], 1)
                dve.wait_ge(s["slow_t"], 1)
                dve.tensor_copy(nT[:].rearrange("p i q -> p (i q)"), ps[:, 0, :].bitcast(bf16)[:, 0:3 * P]).then_inc(s["slow_copied"], 1)

            def stage(t, b):
                if not (isinstance(t, int) and t == 0):
                    dve.wait_ge(s["x_pv"], t * 4 - 3)
                dve.tensor_copy(VX[:, b, :, :, 0:9],
                                (V9[:, t] if isinstance(t, int) else V9[:, bass.ds(t, 1)].rearrange("p o h d -> p (o h) d"))
                                .rearrange("p (j c) d -> p c j d", j=4)).then_inc(s["v_staged"], 1)

            dve.wait_ge(s["v_copied"], NCH + 1 + CREDIT)
            stage(0, 0)
            with dve.Fori(0, (KT - 3) // 2) as i:
                stage(2 * i + 1, 1)
                stage(2 * i + 2, 0)
            stage(KT - 2, 1)
            stage(KT - 1, 0)
            finish(1, s["x_pv"], KT * H // 4)
            if stop == 2:
                return

            norm(2)
            nred = [0]

            def scale_of(src, to, unit=None):
                dve.tensor_reduce(col[:, 8:9], src, AX.XY, ALU.max, apply_absolute_value=True).then_inc(s["am_col"], 1)
                nred[0] += 1
                dve.wait_ge(s["am_all"], nred[0])
                if unit is None:
                    step(dve.tensor_scalar(col[:, to:to + 1], col[:, 9:10], 1.0 / QMAX, 1e-12, ALU.mult, ALU.max))
                    step(dve.reciprocal(col[:, 11:12], col[:, to:to + 1]))
                else:
                    step(dve.tensor_scalar(col[:, 13:14], col[:, 9:10], unit, 1.0 / QMAX, ALU.mult, ALU.mult))
                    step(dve.tensor_scalar(col[:, to:to + 1], col[:, 13:14], 1e-12, None, ALU.max))
                    step(dve.reciprocal(col[:, 13:14], col[:, to:to + 1]))
                    step(dve.tensor_scalar(col[:, 11:12], col[:, 13:14], unit, None, ALU.mult))

            def quantize(t, done=None):
                step(dve.tensor_scalar(t, t, col[:, 11:12], MAGIC, ALU.mult, ALU.add))
                last = dve.tensor_scalar(t, t, MAGIC + QMAX, -MAGIC, ALU.min, ALU.add)
                if done is None:
                    step(last)
                else:
                    last.then_inc(done, 1)

            dve.wait_ge(ln[2]["norm"], 1)
            scale_of(XN[:], 10)
            quantize(XN[:], ln[2]["norm"])
            dve.wait_ge(s["up_copied"], 3)
            scale_of(UP, 12)
            quantize(UP)
            for t in range(3):
                dve.wait_ge(s["gate_ready"], t + 1)
                b = 2 * ((t + 3) % 4)
                step(dve.tensor_scalar(GA[:, t, :], ps[:, b:b + 2, :].rearrange("p b n -> p (b n)"), col[:, 10:11], None, ALU.mult))
            scale_of(GA, 14)
            quantize(GA, s["gate_copied"])
            dve.wait_ge(s["sig_done"], 1)
            step(dve.tensor_scalar(FB, FB, 65536.0, MAGIC, ALU.mult, ALU.add))
            step(dve.tensor_scalar(FB, FB, MAGIC + 65535.0, -MAGIC, ALU.min, ALU.add))
            step(dve.tensor_scalar(col[:, 17:18], col[:, 14:15], 1.0 / 65536.0, None, ALU.mult))
            step(dve.scalar_tensor_tensor(GA, GA, col[:, 17:18], FB, ALU.mult, ALU.mult))
            scale_of(GA, 15)
            quantize(GA)
            step(dve.tensor_tensor(GA, GA, UP, ALU.mult))
            step(dve.tensor_scalar(col[:, 18:19], col[:, 15:16], col[:, 12:13], None, ALU.mult))
            scale_of(GA, 16, unit=col[:, 18:19])
            quantize(GA, s["oq_ready"])
            for half in range(2):
                dve.wait_ge(s["y_ready"], half + 1)
                xs = slice(4 * half, 4 * half + 4)
                dve.scalar_tensor_tensor(XN[:, xs, :], ps[:, half, :].rearrange("p (t d) -> p t d", t=4), col[:, 16:17],
                                         X[:, xs, :], ALU.mult, ALU.add).then_inc(s["x_scaled"], 1)

        @block.tensor
        def _(pe):
            mm = pe.matmul
            pe.wait_ge(s["prep_credit"], len(credited))
            pe.wait_ge(s["consts"], 64)

            def chunk(c, b, n, tiles):
                pe.wait_ge(s["ctxT_ready"], c + 1)
                for t, m in tiles:
                    last = pe.transpose(ps[:, b, t * P:t * P + m], C[0:m, b, t, :], ident[0:m, 0:m])
                last.then_inc(s["ctx_t_ready"], 1)
                pe.wait_ge(s["ctxT_ready"], c + (1 + CREDIT))
                pe.wait_ge(s["k_split"], c + 1)
                mm(ps[:, 2 + b, 0:n], w_k[:], CT[:, b, 0:n], start=True, stop=True).then_inc(s["k_ready"], 1)
                pe.wait_ge(s["v_copied"], c + 1)
                for t, m in tiles:
                    last = mm(ps[0:m, 4 + b, t * P:t * P + P], CT[:, b, t * P:t * P + m], w_v[:], start=True, stop=True)
                last.then_inc(s["v_ready"], 1)
                pe.wait_ge(s["sq_ready"], c + (1 + CREDIT))
                mm(ps[:, 6 + b, 0:n], headsum[:], csq[:, b, 0:n], start=True, stop=True).then_inc(s["n_ready"], 1)

            whole = [(t, P) for t in range(CH)]
            with pe.Fori(0, NCH // 2) as i:
                for b in range(2):
                    pe.wait_ge(ctx_loaded[b], 16 * i + 16)
                    chunk(2 * i + b, b, CH * P, whole)
            pe.wait_ge(s["ctx_tail_loaded"], 32)
            chunk(NCH, 0, REST, [(0, P), (1, P), (2, TAIL)])

            pe.wait_ge(s["w_ready"], 1)
            pe.wait_ge(s["v_copied"], NCH + 1 + CREDIT)
            for g in range(3):
                for t in range(3):
                    last = pe.transpose(ps[:, 5 + g, t * P:t * P + P], wraw[:, 3 * g + t, :], ident[:])
                last.then_inc(s["w_t_ready"], 1)

            def norm_t(k, count=1):
                pe.wait_ge(ln[k]["norm"], count)
                for t in range(NT):
                    last = pe.transpose(ps[:, t // 4, (t % 4) * P:(t % 4) * P + P], XN[:, t, :], ident[:])
                    if t % 4 == 3:
                        last.then_inc(ln[k]["T"], 1)

            norm_t(0)
            pe.wait_ge(s["weights_loaded"], 144)
            pe.wait_ge(s["w_t_copied"], 3)
            for half in range(2):
                pe.wait_ge(ln[0]["copied"], half + 1)
                xt = XT[:, half * 512:half * 512 + 512]
                mm(ps[0:DC, 2 + half, :], w_dq[:], xt, start=True, stop=True).then_inc(s["lat_ready"], 1)
                mm(ps[0:DC, 4 + half, :], w_dkv[:], xt, start=True, stop=True).then_inc(s["lat_ready"], 1)
            pe.wait_ge(s["lat_copied"], 3)
            for half in range(2):
                last = mm(ps[:, half, :], w_uq[:], lat[:, 0, half * 512:half * 512 + 512], start=True, stop=True)
            last.then_inc(s["qk_ready"], 1)
            for half in range(2):
                last = mm(ps[:, 2 + half, :], w_uk[:], lat[:, 1, half * 512:half * 512 + 512], start=True, stop=True)
            last.then_inc(s["qk_ready"], 1)
            for t in range(NT):
                last = mm(ps[:, 6 + t // 4, (t % 4) * P:(t % 4) * P + P], lat[:, 1, t * P:t * P + P], w_uv[:], start=True, stop=True)
                if t % 4 == 3:
                    last.then_inc(s["vs_ready"], 1)

            pe.wait_ge(s["q_spread"], 192)
            pe.wait_ge(s["ks_spread"], 96)
            pe.wait_ge(s["vs_copied"], NT)
            pe.wait_ge(s["qk_copied"], 2)
            pe.wait_ge(s["identb_ready"], 1)
            with pe.Fori(0, NP) as i:
                for v in range(2 * NT):
                    sl, qt = v // NT, v % NT
                    r = 2 * (v % 4)
                    pe.wait_ge(s["m_reduced"], i * (2 * NT) + (v + 1))
                    lhs = QQ[0:ROWS, bass.ds(i * 2 + sl, 1), qt * P:qt * P + P].rearrange("r o q -> r (o q)")
                    n = (qt + 1) * P
                    for b in range((n + 511) // 512):
                        lo, hi = 512 * b, min(n, 512 * b + 512)
                        diag = hi == n
                        last = mm(ps[:, r + b, 0:hi - lo], lhs, KS[:, bass.ds(i, 1), lo:hi].rearrange("r o k -> r (o k)"),
                                  start=True, stop=not diag)
                    last = mm(ps[:, r + b, n - P - lo:n - lo], identb[:], mask[:, 1, :], start=False, stop=True)
                    last.then_inc(s["m_scores"], 1)

            def negs(parts, count, done):
                pe.wait_ge(parts, count)
                for k in range(3):
                    last = pe.transpose(ps[:, 0, :].bitcast(bf16)[:, k * P:k * P + P], npart[:, k, :], identb[:])
                last.then_inc(done, 1)

            negs(s["neg_parts"], 1, s["neg_t"])
            pe.wait_ge(s["neg_rows"], 48)

            def spans(kt):
                return [(g, max(512 * g, kt * P), 512 * g + 512) for g in range(2) if 512 * g + 512 > kt * P]

            def self_scores(u):
                kt, h = divmod(u, H)
                if u >= 2:
                    pe.wait_ge(s["self_exp"], u - 1)
                for g, lo, hi in spans(kt):
                    bank = ps[:, 2 * (u % 2) + g, :]
                    diag = lo == kt * P
                    last = mm(bank[:, lo - 512 * g:hi - 512 * g], KS[:, h // 2, kt * P:kt * P + P], QQ[0:ROWS, h, lo:hi],
                              start=True, stop=not diag)
                    if diag:
                        last = mm(bank[:, lo - 512 * g:lo - 512 * g + P], identb[:], mask[:, 0, :], start=False, stop=True)
                last.then_inc(s["self_ready"], 1)

            def window(v, h):
                c, j = h % 4, h // 4
                flat = v[:, c].rearrange("p j e -> p (j e)")
                return flat[:, 23 * j:23 * j + 32] if j < 3 else flat[:, 96:128]

            def self_pv(u0, g):
                kt = u0 // H
                last = None
                for gg, lo, hi in spans(kt):
                    if gg != g:
                        continue
                    for u in range(u0, u0 + 4):
                        h = u % H
                        c, j = h % 4, h // 4
                        last = mm(ps[32 * c:32 * c + 32, 4 + 2 * (j // 3) + g, lo - 512 * g:hi - 512 * g], window(VS[:, kt], h),
                                  PR[:, u % 8, lo:hi], start=kt == 0 and j in (0, 3), stop=kt == (3 if g == 0 else 7) and j in (2, 3))
                return last

            for u0 in range(0, NT * H + 4, 4):
                for half in range(2):
                    for u in (u0 + 2 * half, u0 + 2 * half + 1):
                        if u < NT * H:
                            self_scores(u)
                    if u0:
                        if u0 == NT * H:
                            pe.wait_ge(s["self_exp"], u0)
                        last = self_pv(u0 - 4, half)
                if u0:
                    last.then_inc(s["self_pv"], 1)

            def finish(k, w):
                pe.wait_ge(fin[k]["oT"], 2)
                for a in range(2):
                    for t in range(NT):
                        last = pe.transpose(ps[:, 2 * a + t // 4, (t % 4) * P:(t % 4) * P + P], OT[:, a, t * P:t * P + P], ident[:])
                last.then_inc(fin[k]["back"], 1)
                pe.wait_ge(fin[k]["attn"], 1)
                for t in range(NT):
                    last = pe.transpose(ps[:, t // 4, (t % 4) * P:(t % 4) * P + P], XN[:, t, :], ident[:])
                    if t % 4 == 3:
                        last.then_inc(fin[k]["attnT"], 1)
                for t in range(NT):
                    pe.wait_ge(fin[k]["attnTc"], t // 4 + 1)
                    last = mm(ps[:, 2 + t // 4, (t % 4) * P:(t % 4) * P + P], XT[:, t * P:t * P + P], w[:], start=True, stop=True)
                last.then_inc(fin[k]["y"], 1)

            finish(0, w_os)
            if stop == 1:
                return
            norm_t(1)
            for half in range(2):
                pe.wait_ge(ln[1]["copied"], half + 1)
                last = mm(ps[:, 4 + half, :], w_q[:], XT[:, half * 512:half * 512 + 512], start=True, stop=True)
            last.then_inc(s["xq_ready"], 1)
            pe.wait_ge(s["xsq"], 1)
            for half in range(2):
                last = mm(ps[:, 6 + half, :], headsum[:], kpart[:, 0, half * 512:half * 512 + 512], start=True, stop=True)
            last.then_inc(s["x_norm"], 1)
            pe.wait_ge(s["xq_spread"], 192)
            pe.wait_ge(s["flag_ready"], 1)
            exact = pe.value_load(flag[0:1, 0:1], min_val=0, max_val=1)
            with pe.If(exact > 0):
                def scan(t, n):
                    with pe.Fori(0, NP) as i:
                        pe.wait_ge(s["slow_loaded"], t * (16 * TERMS) + 16 * TERMS)
                        for sl in range(2):
                            v = t * H + i * 2
                            pe.wait_ge(s["slow_reduced"], (v + sl) * 2 + 1)
                            for qt in range(NT):
                                last = mm(ps[:, 2 * sl + qt // 4, (qt % 4) * P:(qt % 4) * P + n],
                                          QQ[0:ROWS, bass.ds(i * 2 + sl, 1), qt * P:qt * P + P].rearrange("r o q -> r (o q)"),
                                          KX[:, 0, bass.ds(i, 1), 0:n].rearrange("r o k -> r (o k)"), start=True, stop=True)
                            last.then_inc(s["slow_scores"], 1)

                with pe.Fori(0, KT - 1) as t:
                    scan(t, P)
                scan(KT - 1, TAIL)
                negs(s["slow_neg"], 4, s["slow_t"])
                pe.wait_ge(s["slow_rows"], 48)

            for bank in range(4, 8):
                mm(ps[:, bank, :], zeros[0:ROWS, :], QQ[0:ROWS, 0, 0:512], start=True, stop=False)

            def cross_scores(t, h, b):
                if not (isinstance(t, int) and t == 0 and h < 2):
                    pe.wait_ge(s["x_exp"], t * H + (h - 1))
                for g in range(2):
                    last = mm(ps[:, 2 * (h % 2) + g, :], KX[:, b, h // 2, :], QQ[0:ROWS, h, 512 * g:512 * g + 512],
                              start=True, stop=True)
                last.then_inc(s["xs_ready"], 1)

            def cross_pv(h0, b, g, final=False):
                for h in range(h0, h0 + 4):
                    c, j = h % 4, h // 4
                    last = mm(ps[32 * c:32 * c + 32, 4 + 2 * (j // 3) + g, :], window(VX[:, b], h),
                              PR[:, h % 8, 512 * g:512 * g + 512], start=False, stop=final and j in (2, 3))
                return last

            def cross_tile(t, b, loaded, first=False, final=False):
                pe.wait_ge(kx_loaded[b], loaded)
                for h0 in range(0, H, 4):
                    for g in range(2):
                        for h in (h0 + 2 * g, h0 + 2 * g + 1):
                            cross_scores(t, h, b)
                        if h0 == 4 and g == 0:
                            pe.wait_ge(s["v_staged"], t + 1)
                        if h0 or not first:
                            last = cross_pv((h0 - 4) % H, b if h0 else 1 - b, g, final and h0 > 0)
                    if h0 or not first:
                        last.then_inc(s["x_pv"], 1)

            LOAD = 16 * TERMS
            cross_tile(0, 0, LOAD, first=True)
            with pe.Fori(0, (KT - 3) // 2) as i:
                cross_tile(2 * i + 1, 1, i * LOAD + LOAD)
                cross_tile(2 * i + 2, 0, i * LOAD + 2 * LOAD)
            cross_tile(KT - 2, 1, LOAD * ((KT - 1) // 2))
            cross_tile(KT - 1, 0, LOAD * ((KT + 1) // 2), final=True)
            pe.wait_ge(s["x_exp"], KT * H)
            for g in range(2):
                last = cross_pv(H - 4, 0, g, final=True)
            last.then_inc(s["x_pv"], 1)
            finish(1, w_ox)
            if stop == 2:
                return

            norm_t(2, count=2)
            pe.wait_ge(ln[2]["copied"], 2)
            for t in range(3):
                for g in range(2):
                    last = mm(ps[:, 2 * t + g, :], wT[:, 3 + t, :], XT[:, 512 * g:512 * g + 512], start=True, stop=True)
                last.then_inc(s["up_ready"], 1)
            for t in range(3):
                if t:
                    pe.wait_ge(s["up_copied"], t)
                for g in range(2):
                    last = mm(ps[:, 2 * ((t + 3) % 4) + g, :], wT[:, t, :], XT[:, 512 * g:512 * g + 512], start=True, stop=True)
                last.then_inc(s["gate_ready"], 1)
            pe.wait_ge(s["oq_ready"], 1)
            for t in range(NT):
                for k in range(3):
                    last = mm(ps[:, t // 4, (t % 4) * P:(t % 4) * P + P], GA[:, k, t * P:t * P + P], wT[:, 6 + k, :],
                              start=k == 0, stop=k == 2)
                if t % 4 == 3:
                    last.then_inc(s["y_ready"], 1)


_INS = ['x', 'ctx_1024', 'L0_attn_W_dq', 'L0_attn_W_uq', 'L0_attn_W_dkv', 'L0_attn_W_uk', 'L0_attn_W_uv', 'L0_attn_W_o',
        'L0_xattn_Wq', 'L0_xattn_Wk', 'L0_xattn_Wv', 'L0_xattn_Wo', 'L0_ffn_w_gate', 'L0_ffn_w_up', 'L0_ffn_w_down']


def kernel(**inputs):
    import ml_dtypes
    import concourse.bacc as _bacc
    from concourse.bass_utils import run_bass_kernel_spmd as _run

    nc = _bacc.Bacc("TRN2", target_bir_lowering=False, num_devices=1)
    at = np.arange(P)
    masks = np.zeros((P, 2, P), np.float32)
    masks[:, 0, :] = np.where(at[:, None] > at[None, :], MASKED, 0.0)
    masks[:, 1, :] = np.where(at[None, :] > at[:, None], MASKED, 0.0)
    heads = (at[:, None] // DK == at[None, :] // DK)
    arrays, args = {}, []
    for name in _INS:
        a = np.ascontiguousarray(inputs[name])
        arrays[f"in_{name}"] = a
        args.append(nc.dram_tensor(f"in_{name}", a.shape, mybir.dt.from_np(a.dtype), kind="ExternalInput").ap())
    for name, a in (("ident", np.eye(P, dtype=np.float32)), ("masks", masks.astype(ml_dtypes.bfloat16)),
                    ("heads", heads.astype(ml_dtypes.bfloat16))):
        arrays[f"const_{name}"] = a
        args.append(nc.dram_tensor(f"const_{name}", a.shape, mybir.dt.from_np(a.dtype), kind="ExternalInput").ap())
    args.append(nc.dram_tensor("out", (1, S, D), mybir.dt.float32, kind="ExternalOutput").ap())
    build(nc, *args)
    r = _run(nc, [arrays], core_ids=[0])
    return r.results[0]["out"]
```

```python
from contextlib import ExitStack

import numpy as np

import concourse.bass as bass
from concourse import mybir

S, SC, D, H, DK, DC, FF = 1024, 6404, 128, 16, 8, 32, 384
P = 128
NT = S // P
NP = H // 2
KT = SC // P + 1
TAIL = SC - (KT - 1) * P
CH = 4
NCH = KT // CH
REST = SC - NCH * CH * P
KPART = (0, 0, 0, 1, 1, 2)
QPART = (0, 1, 2, 0, 1, 0)
TERMS = len(KPART)
SHIFT, ROWS = 96, 100
HALF = 512
UNITS = NP
BLK = 32
QMAX, WMAX = 32767.0, 7.0
MAGIC = 1.5 * 2.0 ** 23
MASKED = -1.0e38
SAFE = 40.0
EPS = 1e-5


def build(nc, x, ctx, wdq, wuq, wdkv, wuk, wuv, wo_s, wq, wk, wv, wo_x, wg, wu, wd,
          ident_in, mask_in, heads_in, out, force_exact=False, stop=9):
    f32, bf16, i32 = mybir.dt.float32, mybir.dt.bfloat16, mybir.dt.int32
    ALU, ACT, AX = mybir.AluOpType, mybir.ActivationFunctionType, mybir.AxisListType
    ABSMAX = bass.bass_isa.ReduceOp.absmax

    st = ExitStack()
    with st:
        def sb(name, shape, dt=f32):
            return st.enter_context(nc.sbuf_tensor(name, shape, dt))

        def sem(name):
            return st.enter_context(nc.semaphore(name))

        q_dram = nc.dram_tensor("q_parts", (2, 3, P, S), bf16, kind="Internal").ap()
        ks_dram = nc.dram_tensor("self_k_parts", (3, P, S), bf16, kind="Internal").ap()
        kx_dram = nc.dram_tensor("ctx_k_parts", (3, P, KT * P), bf16, kind="Internal").ap()

        ident = sb("ident", [P, P])
        identb = sb("identb", [P, P], bf16)
        mask = sb("mask", [P, 2, P], bf16)
        headsum = sb("headsum", [P, P], bf16)
        zeros = sb("zeros", [P, P], bf16)
        eps = sb("eps", [P, 1])
        w_dq = sb("w_dq", [D, DC])
        w_uq = sb("w_uq", [DC, D])
        w_dkv = sb("w_dkv", [D, DC])
        w_uk = sb("w_uk", [DC, D])
        w_uv = sb("w_uv", [DC, D])
        w_os = sb("w_os", [D, D])
        w_q = sb("w_q", [D, D])
        w_k = sb("w_k", [D, D])
        w_v = sb("w_v", [D, D])
        w_ox = sb("w_ox", [D, D])
        wraw = sb("wraw", [P, 9, P])
        wmax = sb("wmax", [P, 36])
        wscale = sb("wscale", [P, 36])
        wT = sb("wT", [P, 9, P])

        X = sb("X", [P, NT, D])
        XN = sb("XN", [P, NT, D])
        XT = sb("XT", [D, S])
        stats = sb("stats", [P, NT, 6])
        moments = sb("moments", [P, NT, 2])
        std = sb("std", [P, NT])
        rstd = sb("rstd", [P, NT])
        part = sb("part", [P, 3, S], bf16)
        kpart = sb("kpart", [P, 3, S], bf16)
        QQ = sb("QQ", [P, H, S], bf16)
        KS = sb("KS", [ROWS, NP, S], bf16)
        KX = sb("KX", [ROWS, 3, NP, P], bf16)
        VS = sb("VS", [P, NT, 4, 4, 32])
        V9 = sb("V9", [P, KT, H, 9])
        VX = sb("VX", [P, 3, 4, 4, 32])
        PR = sb("PR", [P, 8, 2, HALF])
        OT = sb("OT", [P, 2, S])
        rec = sb("rec", [P, 4, NT, 4])
        mx = sb("mx", [P, H * NT])
        mtmp = sb("mtmp", [P, NT])
        npart = sb("npart", [P, 3, H * NT], bf16)
        nrem = sb("nrem", [P, H * NT])
        nT = sb("nT", [P, 3, P], bf16)
        C = sb("C", [P, 2, CH, D])
        CT = sb("CT", [D, 2, CH * P])
        cpart = sb("cpart", [P, 2, 3, CH * P], bf16)
        col = sb("col", [P, 24])
        flag = sb("flag", [1, 1], i32)
        ps = st.enter_context(nc.psum_tensor("ps", [P, 8, HALF], f32))

        prf = PR[:].rearrange("p u a n -> p u (a n)")
        lat = prf[0:DC, 0:2, :]
        crem, kf = prf[:, 2, 0:HALF], prf[:, 3, 0:HALF]
        csq = prf[:, 2, HALF:S].bitcast(bf16)[:, 0:HALF]
        NK = PR[:, 4:8, :, :].bitcast(bf16).rearrange("p u a n -> p (u a n)")[:, 0:SC]
        rem, qf = OT[:, 0, :], OT[:, 1, :]
        UP, GA = prf[:, 0:3, :], prf[:, 3:6, :]
        FB = QQ[:, 0:6, :].bitcast(f32).rearrange("p (t a) s -> p t (a s)", t=3)
        wb = wraw[:].rearrange("p t (b i) -> p (t b) i", i=BLK)
        sc, winv = (w[:].rearrange("p (b o) -> p b o", o=1).to_broadcast([P, 36, BLK]) for w in (wscale, wmax))

        names = """consts x_loaded weights_loaded ffn_w_loaded ctx_tail_loaded identb_ready
            ctx_t_ready ctxT_ready k_ready k_copied k_rem k_part2 k_sq k_parts k_tail_stored v_ready v_copied n_ready n_copied
            w_ready w_t_ready w_t_copied pool_step pool_init dve_step q_stored q_spread ks_stored ks_spread
            lat_ready lat_copied qk_ready qk_first qk_parts vs_ready vs_copied m_scores m_reduced neg_parts neg_t neg_copied
            neg_rows self_ready self_exp self_pv self_out q_cleared xq_ready xq_first xq_parts xsq x_norm xq_stored xq_spread
            bound_col bound_all bound_root flag_ready slow_loaded slow_scores slow_reduced slow_neg slow_t slow_copied
            slow_rows xs_ready x_exp x_pv x_out v_staged am_col am_all up_ready up_copied gate_ready gate_copied sig_done
            oq_ready y_ready y_done out_stored""".split()
        s = {n: sem(n) for n in names}
        ctx_loaded = [sem(f"ctx_loaded{b}") for b in range(2)]
        kx_loaded = [sem(f"kx_loaded{b}") for b in range(3)]
        k_stored = sem("k_stored")
        ln = [{n: sem(f"ln{k}_{n}") for n in ("var", "std", "norm", "T", "copied")} for k in range(3)]
        fin = [{n: sem(f"fin{k}_{n}") for n in ("back", "attn", "attnT", "attnTc", "y", "res")} for k in range(2)]
        granted = ("ctxT_ready", "k_copied", "k_rem", "v_copied", "n_copied")
        GRANT = 1

        def fill_keys(eng, dst, src, done):
            for i, part_no in enumerate(KPART):
                eng.dma_start(dst[i * 16:i * 16 + 16], src(part_no).rearrange("(p r) n -> r p n", r=16)).then_inc(done, 16)

        def fill_queries(eng, k, done):
            for i, part_no in enumerate(QPART):
                for slot in range(2):
                    r = i * 16 + slot * 8
                    eng.dma_start(QQ[r:r + 8, slot:H:2, :],
                                  q_dram[k, part_no].rearrange("(p s d) n -> s d p n", s=2, d=DK)[slot]).then_inc(done, 16)

        def fill_shift(eng, done):
            for i in range(3):
                eng.dma_start(QQ[SHIFT + i:SHIFT + i + 1, :, :].rearrange("o h (t q) -> o (h t) q", q=P),
                              nT[:, i, :]).then_inc(done, 16)

        def self_units():
            return [(qb, kt, p) for qb in range(2) for kt in range(4 * qb + 4) for p in range(NP)]

        def first_query(qb, kt):
            return max(0, kt * P - qb * HALF)

        block = st.enter_context(nc.Block())

        @block.sync
        def _(sp):
            def load_chunk(c, b):
                src = ctx[0, 0:NCH * CH * P, :].rearrange("(c t p) d -> c p t d", p=P, t=CH)[bass.ds(c, 1)]
                sp.dma_start(C[:, b, :, :], src.rearrange("c p t d -> p (c t) d")).then_inc(ctx_loaded[b], 16)

            sp.dma_start(X[:], x[0].rearrange("(t p) d -> p t d", p=P)).then_inc(s["x_loaded"], 16)
            sp.dma_start(ident[:], ident_in).then_inc(s["consts"], 16)
            for dst, src in ((w_dq, wdq), (w_dkv, wdkv), (w_uq, wuq), (w_uk, wuk), (w_uv, wuv)):
                sp.dma_start(dst[:], src).then_inc(s["weights_loaded"], 16)
            sp.dma_start(mask[:], mask_in).then_inc(s["weights_loaded"], 16)
            for k, w in enumerate((wg, wu)):
                sp.dma_start(wraw[:, 3 * k:3 * k + 3, :], w.rearrange("(t p) i -> p t i", p=P)).then_inc(s["ffn_w_loaded"], 16)
            sp.dma_start(wraw[:, 6:9, :], wd.rearrange("o (t i) -> o t i", i=P)).then_inc(s["ffn_w_loaded"], 16)
            for dst, src in ((w_k, wk), (w_v, wv), (w_q, wq)):
                sp.dma_start(dst[:], src.rearrange("d n h -> d (n h)")).then_inc(s["weights_loaded"], 16)
            sp.dma_start(headsum[:], heads_in).then_inc(s["weights_loaded"], 16)
            sp.dma_start(w_ox[:], wo_x.rearrange("n h d -> (n h) d")).then_inc(s["weights_loaded"], 16)
            sp.dma_start(w_os[:], wo_s).then_inc(s["weights_loaded"], 16)
            for b in range(2):
                load_chunk(b, b)

            sp.wait_ge(s["qk_parts"], 1)
            sp.dma_start(ks_dram.rearrange("i p n -> p i n"), kpart[:]).then_inc(s["ks_stored"], 16)
            sp.wait_ge(s["qk_parts"], 2)
            sp.dma_start(q_dram[0].rearrange("i p n -> p i n"), part[:]).then_inc(s["q_stored"], 16)
            sp.wait_ge(s["pool_init"], 1)
            sp.wait_ge(s["ks_stored"], 16)
            fill_keys(sp, KS[:], lambda k: ks_dram[k], s["ks_spread"])
            sp.wait_ge(s["q_stored"], 16)
            fill_queries(sp, 0, s["q_spread"])

            with sp.Fori(1, NCH // 2) as i:
                for b in range(2):
                    sp.wait_ge(s["ctx_t_ready"], 2 * i + (b - 1))
                    load_chunk(2 * i + b, b)
            sp.wait_ge(s["ctx_t_ready"], NCH - 1)
            lo = NCH * CH * P
            sp.dma_start(C[:, 0, 0:2, :], ctx[0, lo:lo + 2 * P, :].rearrange("(t p) d -> p t d", p=P)).then_inc(s["ctx_tail_loaded"], 16)
            sp.dma_start(C[0:TAIL, 0, 2, :], ctx[0, lo + 2 * P:SC, :]).then_inc(s["ctx_tail_loaded"], 16)
            sp.wait_ge(s["neg_copied"], 1)
            fill_shift(sp, s["neg_rows"])

            def load_keys(t, n, b, done):
                fill_keys(sp, KX[:, b, :, 0:n], lambda k: kx_dram[k, :, bass.ds(t * P, n)], done)

            sp.wait_ge(k_stored, 16 * NCH)
            sp.wait_ge(s["k_tail_stored"], 16)
            for t in range(3):
                load_keys(t, P, t, kx_loaded[t])
            sp.wait_ge(s["xq_parts"], 1)
            sp.dma_start(q_dram[1].rearrange("i p n -> p i n"), part[:]).then_inc(s["xq_stored"], 16)
            sp.wait_ge(s["xq_stored"], 16)
            fill_queries(sp, 1, s["xq_spread"])

            sp.wait_ge(s["flag_ready"], 1)
            exact = sp.value_load(flag[0:1, 0:1], min_val=0, max_val=1)
            with sp.If(exact > 0):
                with sp.Fori(1, KT - 1) as t:
                    sp.wait_ge(s["slow_scores"], t * H)
                    load_keys(t, P, 0, s["slow_loaded"])
                sp.wait_ge(s["slow_scores"], (KT - 1) * H)
                load_keys(KT - 1, TAIL, 0, s["slow_loaded"])
                sp.wait_ge(s["slow_scores"], KT * H)
                load_keys(0, P, 0, s["slow_loaded"])
                sp.wait_ge(s["slow_copied"], 1)
                fill_shift(sp, s["slow_rows"])

            def reload_keys(step, t, n, b):
                sp.wait_ge(s["xs_ready"], step * UNITS - 2 * UNITS)
                load_keys(t, n, b, kx_loaded[b])

            for qb in range(2):
                if qb:
                    for t in range(3):
                        reload_keys(KT + t, t, P, t)
                with sp.Fori(1, KT // 3 - 1) as i:
                    for r in range(3):
                        reload_keys(3 * i + (qb * KT + r), 3 * i + r, P, r)
                for t in range(KT - 3, KT):
                    reload_keys(qb * KT + t, t, P if t < KT - 1 else TAIL, t % 3)
            ov = out[0].rearrange("(t p) d -> p t d", p=P)
            for half in range(2):
                sp.wait_ge(s["y_done"], half + 1)
                sp.dma_start(ov[:, 4 * half:4 * half + 4, :], XN[:, 4 * half:4 * half + 4, :]).then_inc(s["out_stored"], 16)
            sp.wait_ge(s["out_stored"], 32)

        @block.gpsimd
        def _(pool):
            steps = [0]

            def step(ins):
                steps[0] += 1
                ins.then_inc(s["pool_step"], 1)
                pool.wait_ge(s["pool_step"], steps[0])

            step(pool.memset(eps[:], EPS))
            for n in granted:
                pool.memset(zeros[:], 0.0).then_inc(s[n], GRANT)
                pool.wait_ge(s[n], GRANT)
            pool.memset(zeros[:], 0.0).then_inc(s["m_reduced"], 2)
            pool.wait_ge(s["m_reduced"], 2)
            step(pool.memset(KS[SHIFT:ROWS], 0.0))
            step(pool.memset(KS[SHIFT:ROWS - 1], 1.0))
            step(pool.memset(QQ[SHIFT:ROWS, :, :], 1.0))
            step(pool.memset(QQ[SHIFT:ROWS - 1, :, :].bitcast(i32), 0))
            pool.memset(QQ[0:SHIFT, :, :].bitcast(i32), 0).then_inc(s["pool_init"], 1)
            pool.wait_ge(s["pool_init"], 1)
            step(pool.memset(VS[:], 0.0))
            step(pool.memset(VS[:, :, :, :, 8:9], 1.0))
            step(pool.memset(V9[:, 0:KT - 1, :, 8:9], 1.0))
            step(pool.memset(V9[:, KT - 1, :, :], 0.0))
            step(pool.memset(V9[0:TAIL, KT - 1, :, 8:9], 1.0))
            step(pool.memset(VX[:], 0.0))
            step(pool.memset(KX[SHIFT:ROWS], 1.0))

            kv = kx_dram.rearrange("i p n -> p i n")

            def key_parts(c, b, n, stored, count):
                pool.wait_ge(s["k_copied"], c + (1 + GRANT))
                pool.tensor_tensor(crem[:, 0:n], kf[:, 0:n], cpart[:, b, 0, 0:n], ALU.subtract).then_inc(s["k_rem"], 1)
                pool.tensor_tensor(csq[:, 0:n], cpart[:, b, 0, 0:n], cpart[:, b, 0, 0:n], ALU.mult).then_inc(s["k_sq"], 1)
                pool.wait_ge(s["k_part2"], c + 1)
                pool.tensor_tensor(cpart[:, b, 2, 0:n], crem[:, 0:n], cpart[:, b, 1, 0:n], ALU.subtract).then_inc(s["k_parts"], 1)
                pool.wait_ge(s["k_parts"], c + 1)
                pool.dma_start(kv[:, :, bass.ds(c * (CH * P), n)], cpart[:, b, :, 0:n]).then_inc(stored, 16)
                pool.wait_ge(stored, count)

            with pool.Fori(0, NCH // 2) as i:
                for b in range(2):
                    key_parts(2 * i + b, b, CH * P, k_stored, i * 32 + (16 * b + 16))
            key_parts(NCH, 0, REST, s["k_tail_stored"], 16)
            pool.wait_ge(s["self_ready"], len(self_units()))
            pool.memset(QQ[SHIFT:ROWS - 1, :, :].bitcast(i32), 0).then_inc(s["q_cleared"], 1)
            pool.wait_ge(s["q_cleared"], 1)
            pool.wait_ge(s["bound_col"], 1)
            pool.partition_all_reduce(col[:, 2:3], col[:, 1:2], P, ABSMAX).then_inc(s["bound_all"], 1)
            for k in range(5):
                pool.wait_ge(s["am_col"], k + 1)
                pool.partition_all_reduce(col[:, 9:10], col[:, 8:9], P, ABSMAX).then_inc(s["am_all"], 1)

        @block.scalar
        def _(act):
            def norm(k):
                act.wait_ge(ln[k]["var"], 1)
                act.activation(std[:], moments[:, :, 1:2].rearrange("p t o -> p (t o)"), ACT.Sqrt, bias=eps[:]).then_inc(ln[k]["std"], 1)
                for half in range(2):
                    act.wait_ge(ln[k]["T"], half + 1)
                    act.activation(XT[:, half * 512:half * 512 + 512], ps[:, half, :], ACT.Copy).then_inc(ln[k]["copied"], 1)

            act.wait_ge(s["pool_step"], 1)
            norm(0)
            for half in range(2):
                act.wait_ge(s["lat_ready"], 2 * half + 1)
                act.activation(lat[:, 1, half * 512:half * 512 + 512], ps[0:DC, 4 + half, :], ACT.Copy).then_inc(s["lat_copied"], 1)
            act.wait_ge(s["qk_ready"], 1)
            act.activation(kpart[:, 0, :], ps[:, 2:4, :].rearrange("p b n -> p (b n)"), ACT.Copy).then_inc(s["qk_first"], 1)
            act.wait_ge(s["qk_ready"], 2)
            act.activation(qf, ps[:, 0:2, :].rearrange("p b n -> p (b n)"), ACT.Copy, scale=DK ** -0.5)
            act.activation(part[:, 0, :], ps[:, 0:2, :].rearrange("p b n -> p (b n)"), ACT.Copy, scale=DK ** -0.5).then_inc(s["qk_first"], 1)
            act.wait_ge(s["pool_step"], 7)
            for t in range(NT):
                act.wait_ge(s["vs_ready"], t // 4 + 1)
                act.activation(VS[:, t, :, :, 0:8],
                               ps[:, 6 + t // 4, (t % 4) * P:(t % 4) * P + P].rearrange("p (j c d) -> p c j d", j=4, d=DK),
                               ACT.Copy).then_inc(s["vs_copied"], 1)

            def chunk(c, b, n, values):
                act.wait_ge(s["ctx_t_ready"], c + 1)
                act.activation(CT[:, b, 0:n], ps[:, 4, 0:n], ACT.Copy).then_inc(s["ctxT_ready"], 1)
                act.wait_ge(s["k_ready"], c + 1)
                act.wait_ge(s["k_rem"], c + GRANT)
                act.activation(kf[:, 0:n], ps[:, 5, 0:n], ACT.Copy)
                act.activation(cpart[:, b, 0, 0:n], ps[:, 5, 0:n], ACT.Copy).then_inc(s["k_copied"], 1)
                act.wait_ge(s["k_rem"], c + (1 + GRANT))
                act.activation(cpart[:, b, 1, 0:n], crem[:, 0:n], ACT.Copy).then_inc(s["k_part2"], 1)
                act.wait_ge(s["v_ready"], c + 1)
                values()
                act.wait_ge(s["n_ready"], c + 1)
                act.activation(NK[:, bass.ds(c * (CH * P), n)], ps[:, 7, 0:n], ACT.Copy).then_inc(s["n_copied"], 1)

            act.wait_ge(s["pool_step"], 10)
            with act.Fori(0, NCH // 2) as i:
                for b in range(2):
                    def values():
                        act.activation(V9[:, bass.ds((2 * i + b) * CH, CH), :, 0:8],
                                       ps[:, 6, :].rearrange("p (t h d) -> p t h d", t=CH, d=DK), ACT.Copy).then_inc(s["v_copied"], 1)
                    chunk(2 * i + b, b, CH * P, values)

            def last_values():
                act.activation(V9[:, KT - 3:KT - 1, :, 0:8],
                               ps[:, 6, 0:2 * P].rearrange("p (t h d) -> p t h d", t=2, d=DK), ACT.Copy)
                act.activation(V9[0:TAIL, KT - 1, :, 0:8], ps[0:TAIL, 6, 2 * P:3 * P].rearrange("p (h d) -> p h d", d=DK),
                               ACT.Copy).then_inc(s["v_copied"], 1)
            chunk(NCH, 0, REST, last_values)
            for g in range(3):
                act.wait_ge(s["w_t_ready"], g + 1)
                act.activation(wT[:, 3 * g:3 * g + 3, :], ps[:, 4 + g, 0:3 * P].rearrange("p (t i) -> p t i", i=P),
                               ACT.Copy).then_inc(s["w_t_copied"], 1)

            act.wait_ge(s["k_parts"], NCH + 1)
            for u, (qb, kt, p) in enumerate(self_units()):
                lo = first_query(qb, kt)
                act.wait_ge(s["self_ready"], u + 1)
                if u % 2 == 0 and u >= 8:
                    act.wait_ge(s["self_pv"], u // 2 - 3)
                b = 2 * (u % 3)
                act.activation(PR[:, u % 8, :, lo:HALF], ps[:, b:b + 2, lo:HALF], ACT.Exp).then_inc(s["self_exp"], 1)

            def finish(k):
                for half in range(2):
                    act.wait_ge(fin[k]["attnT"], half + 1)
                    act.activation(XT[:, half * 512:half * 512 + 512], ps[:, half, :], ACT.Copy).then_inc(fin[k]["attnTc"], 1)

            finish(0)
            norm(1)
            act.wait_ge(s["xq_ready"], 1)
            act.activation(part[:, 0, :], ps[:, 4:6, :].rearrange("p b n -> p (b n)"), ACT.Copy, scale=DK ** -0.5)
            act.activation(qf, ps[:, 4:6, :].rearrange("p b n -> p (b n)"), ACT.Copy, scale=DK ** -0.5).then_inc(s["xq_first"], 1)
            act.wait_ge(s["bound_all"], 1)
            act.activation(col[:, 3:4], col[:, 2:3], ACT.Sqrt).then_inc(s["bound_root"], 1)

            def exp_tile(base, r, start=False):
                for p in range(UNITS):
                    act.wait_ge(s["xs_ready"], base + (p + 1))
                    if p % 2 == 0 and not start:
                        act.wait_ge(s["x_pv"], half_of(base) + (p // 2 - 3))
                    b = 2 * ((UNITS * r + p) % 3)
                    act.activation(PR[:, p, :, :], ps[:, b:b + 2, :], ACT.Exp).then_inc(s["x_exp"], 1)

            for qb in range(2):
                for r in range(3):
                    base = (qb * KT + r) * UNITS
                    half_of = lambda v: v // 2
                    exp_tile(base, r, start=base == 0)
                with act.Fori(1, KT // 3) as i:
                    for r in range(3):
                        half_of = lambda v: i * (3 * UNITS // 2) + (qb * KT + r) * UNITS // 2
                        exp_tile(i * (3 * UNITS) + (qb * KT + r) * UNITS, r)
            finish(1)
            norm(2)
            for t in range(3):
                act.wait_ge(s["up_ready"], t + 1)
                act.activation(UP[:, t, :], ps[:, 2 * t:2 * t + 2, :].rearrange("p b n -> p (b n)"), ACT.Copy,
                               scale=col[:, 10:11]).then_inc(s["up_copied"], 1)
            act.wait_ge(s["gate_copied"], 1)
            act.activation(FB, GA, ACT.Sigmoid, scale=col[:, 14:15]).then_inc(s["sig_done"], 1)

        @block.vector
        def _(dve):
            steps = [0]

            def step(ins):
                steps[0] += 1
                ins.then_inc(s["dve_step"], 1)
                dve.wait_ge(s["dve_step"], steps[0])

            def norm(k):
                for t in range(NT):
                    last = dve.bn_stats(stats[:, t, :], X[:, t, :])
                step(last)
                for t in range(NT):
                    last = dve.bn_aggr(moments[:, t, :], stats[:, t, :])
                last.then_inc(ln[k]["var"], 1)
                dve.wait_ge(ln[k]["std"], 1)
                step(dve.reciprocal(rstd[:], std[:]))
                for t in range(NT):
                    last = dve.tensor_scalar(XN[:, t, :], X[:, t, :], moments[:, t, 0:1], rstd[:, t:t + 1],
                                             ALU.subtract, ALU.mult)
                last.then_inc(ln[k]["norm"], 1)

            def other_parts(dst, src, done):
                step(dve.tensor_tensor(rem, src, dst[:, 0, :], ALU.subtract))
                step(dve.tensor_copy(dst[:, 1, :], rem))
                dve.tensor_tensor(dst[:, 2, :], rem, dst[:, 1, :], ALU.subtract).then_inc(done, 1)

            dve.wait_ge(s["x_loaded"], 16)
            norm(0)
            dve.wait_ge(s["consts"], 16)
            dve.tensor_copy(identb[:], ident[:]).then_inc(s["identb_ready"], 1)
            for half in range(2):
                dve.wait_ge(s["lat_ready"], 2 * half + 2)
                last = dve.tensor_copy(lat[:, 0, half * 512:half * 512 + 512], ps[0:DC, 2 + half, :])
            last.then_inc(s["lat_copied"], 1)
            dve.wait_ge(s["qk_first"], 1)
            other_parts(kpart[:], ps[:, 2:4, :].rearrange("p b n -> p (b n)"), s["qk_parts"])
            dve.wait_ge(s["qk_parts"], 1)
            dve.wait_ge(s["qk_first"], 2)
            other_parts(part[:], qf, s["qk_parts"])

            dve.wait_ge(s["ffn_w_loaded"], 48)
            step(dve.tensor_reduce(wmax[:], wb, AX.X, ALU.max, apply_absolute_value=True))
            step(dve.tensor_scalar(wscale[:], wmax[:], 1.0 / WMAX, 1e-12, ALU.mult, ALU.max))
            step(dve.reciprocal(wmax[:], wscale[:]))
            step(dve.tensor_tensor(wb, wb, winv, ALU.mult))
            step(dve.tensor_scalar(wraw[:], wraw[:], MAGIC, -MAGIC, ALU.add, ALU.add))
            step(dve.tensor_scalar(wraw[:], wraw[:], -WMAX - 1.0, WMAX, ALU.max, ALU.min))
            dve.tensor_tensor(wb, wb, sc, ALU.mult).then_inc(s["w_ready"], 1)

            with dve.Fori(0, NP) as i:
                for v in range(2 * NT):
                    dve.wait_ge(s["m_scores"], i * (2 * NT) + (v + 1))
                    b = 2 * (v % 2)
                    dve.reduce_max(mx[:, bass.ds(i * (2 * NT) + v, 1)],
                                   ps[:, b:b + 2, :].rearrange("p b n -> p (b n)")[:, 0:(v % NT + 1) * P], AX.X).then_inc(s["m_reduced"], 1)
            dve.wait_ge(s["m_reduced"], H * NT + 2)
            step(dve.tensor_scalar(npart[:, 0, :], mx[:], -1.0, None, ALU.mult))
            step(dve.scalar_tensor_tensor(nrem[:], mx[:], -1.0, npart[:, 0, :], ALU.mult, ALU.subtract))
            step(dve.tensor_copy(npart[:, 1, :], nrem[:]))
            dve.tensor_tensor(npart[:, 2, :], nrem[:], npart[:, 1, :], ALU.subtract).then_inc(s["neg_parts"], 1)
            dve.wait_ge(s["neg_t"], 1)
            dve.tensor_copy(nT[:].rearrange("p i q -> p (i q)"), ps[:, 0, :].bitcast(bf16)[:, 0:3 * P]).then_inc(s["neg_copied"], 1)
            dve.wait_ge(s["n_copied"], NCH + 1 + GRANT)
            dve.reduce_max(col[:, 0:1], NK, AX.X).then_inc(s["n_copied"], 1)

            def evacuate(pv, groups, qb, done):
                dve.wait_ge(pv, groups)
                dve.tensor_copy(OT[:, :, qb * HALF:qb * HALF + HALF], ps[:, 6:8, :]).then_inc(done, 1)

            def finish(k):
                dve.wait_ge(fin[k]["back"], 1)
                view = [ps[:, b0:b0 + 2, :].rearrange("p b (t r) -> p (b t) r", r=P).rearrange("p t (c r) -> p t c r", c=4)
                        for b0 in (0, 2)]
                place = [view[j // 3][:, :, :, 9 * (j % 3):9 * (j % 3) + 9] for j in range(4)]
                for j in range(4):
                    last = dve.reciprocal(rec[:, j, :, :], place[j][:, :, :, 8:9].rearrange("p t c o -> p t (c o)"))
                step(last)
                for j in range(4):
                    o = XN[:, :, j * 32:j * 32 + 32].rearrange("p t (c d) -> p t c d", c=4)
                    last = dve.tensor_tensor(o, place[j][:, :, :, 0:8],
                                             rec[:, j, :, :].rearrange("p t (c o) -> p t c o", o=1).to_broadcast([P, NT, 4, DK]), ALU.mult)
                last.then_inc(fin[k]["attn"], 1)
                dve.wait_ge(fin[k]["y"], 1)
                dve.tensor_tensor(X[:].rearrange("p t d -> p (t d)"), X[:].rearrange("p t d -> p (t d)"),
                                  ps[:, 2:4, :].rearrange("p b n -> p (b n)"), ALU.add).then_inc(fin[k]["res"], 1)
                dve.wait_ge(fin[k]["res"], 1)

            evacuate(s["self_pv"], 16, 0, s["self_out"])
            evacuate(s["self_pv"], 48, 1, s["self_out"])
            finish(0)
            norm(1)
            dve.wait_ge(s["xq_first"], 1)
            dve.tensor_tensor(kpart[:, 0, :], part[:, 0, :], part[:, 0, :], ALU.mult).then_inc(s["xsq"], 1)
            other_parts(part[:], qf, s["xq_parts"])
            dve.wait_ge(s["x_norm"], 1)
            step(dve.reduce_max(col[:, 4:5], ps[:, 6:8, :].rearrange("p b n -> p (b n)"), AX.X))
            dve.tensor_scalar(col[:, 1:2], col[:, 4:5], col[:, 0:1], 1.03, ALU.mult, ALU.mult).then_inc(s["bound_col"], 1)
            dve.wait_ge(s["bound_root"], 1)
            step(dve.tensor_scalar(col[:, 4:5], col[:, 3:4], -1.0 if force_exact else SAFE, None, ALU.is_gt))
            step(dve.tensor_copy(flag[:], col[0:1, 4:5]))
            step(dve.tensor_scalar(col[:, 5:6], col[:, 4:5], -1.0, 1.0, ALU.mult, ALU.add))
            step(dve.scalar_tensor_tensor(col[:, 6:7], col[:, 3:4], -1.0, col[:, 5:6], ALU.mult, ALU.mult))
            step(dve.tensor_scalar(col[:, 6:7], col[:, 6:7], -1.0, None, ALU.add))
            step(dve.tensor_scalar(col[:, 7:8], ident[:, ROWS - 1:ROWS], col[:, 6:7], 1.0, ALU.mult, ALU.add))
            dve.wait_ge(s["pool_step"], 12)
            rows = KX[SHIFT:ROWS].rearrange("r b p n -> r (b p n)")
            dve.tensor_scalar(rows, rows, col[SHIFT:ROWS, 7:8], None, ALU.mult).then_inc(s["flag_ready"], 1)
            dve.wait_ge(s["flag_ready"], 1)
            exact = dve.value_load(flag[0:1, 0:1], min_val=0, max_val=1)
            with dve.If(exact > 0):
                dve.memset(mx[:], -3.0e38).then_inc(s["slow_reduced"], 4)

                def fold(t, n):
                    with dve.Fori(0, NP) as i:
                        for sl in range(2):
                            v = t * H + i * 2
                            dve.wait_ge(s["slow_scores"], v + (sl + 1))
                            dve.wait_ge(s["slow_reduced"], (v + sl) * 2 + 4)
                            dve.tensor_reduce(mtmp[:], ps[:, 2 * sl:2 * sl + 2, :].rearrange("p b (t n) -> p (b t) n", n=P)[:, :, 0:n],
                                              AX.X, ALU.max).then_inc(s["slow_reduced"], 1)
                            dve.wait_ge(s["slow_reduced"], (v + sl) * 2 + 5)
                            m = mx[:, bass.ds(i * (2 * NT) + sl * NT, NT)]
                            dve.tensor_tensor(m, m, mtmp[:], ALU.max).then_inc(s["slow_reduced"], 1)

                with dve.Fori(0, KT - 1) as t:
                    fold(t, P)
                fold(KT - 1, TAIL)
                dve.wait_ge(s["slow_reduced"], 2 * KT * H + 4)
                dve.tensor_scalar(npart[:, 0, :], mx[:], -1.0, None, ALU.mult).then_inc(s["slow_neg"], 1)
                dve.wait_ge(s["slow_neg"], 1)
                dve.scalar_tensor_tensor(nrem[:], mx[:], -1.0, npart[:, 0, :], ALU.mult, ALU.subtract).then_inc(s["slow_neg"], 1)
                dve.wait_ge(s["slow_neg"], 2)
                dve.tensor_copy(npart[:, 1, :], nrem[:]).then_inc(s["slow_neg"], 1)
                dve.wait_ge(s["slow_neg"], 3)
                dve.tensor_tensor(npart[:, 2, :], nrem[:], npart[:, 1, :], ALU.subtract).then_inc(s["slow_neg"], 1)
                dve.wait_ge(s["slow_t"], 1)
                dve.tensor_copy(nT[:].rearrange("p i q -> p (i q)"), ps[:, 0, :].bitcast(bf16)[:, 0:3 * P]).then_inc(s["slow_copied"], 1)

            def stage(step_no, src, r):
                if step_no is not None:
                    dve.wait_ge(s["x_pv"], step_no * 4 - 8)
                dve.tensor_copy(VX[:, r, :, :, 0:9], src.rearrange("p (j c) d -> p c j d", j=4)).then_inc(s["v_staged"], 1)

            for qb in range(2):
                for t in range(3):
                    stage(KT + t if qb else None, V9[:, t, :, :], t)
                with dve.Fori(1, KT // 3) as i:
                    for r in range(3):
                        stage(3 * i + (qb * KT + r), V9[:, bass.ds(3 * i + r, 1), :, :].rearrange("p o h d -> p (o h) d"), r)
                evacuate(s["x_pv"], (qb + 1) * KT * UNITS // 2, qb, s["x_out"])
            finish(1)

            norm(2)
            nred = [0]

            def scale_of(src, to, unit=None):
                dve.tensor_reduce(col[:, 8:9], src, AX.XY, ALU.max, apply_absolute_value=True).then_inc(s["am_col"], 1)
                nred[0] += 1
                dve.wait_ge(s["am_all"], nred[0])
                if unit is None:
                    step(dve.tensor_scalar(col[:, to:to + 1], col[:, 9:10], 1.0 / QMAX, 1e-12, ALU.mult, ALU.max))
                    step(dve.reciprocal(col[:, 11:12], col[:, to:to + 1]))
                else:
                    step(dve.tensor_scalar(col[:, 13:14], col[:, 9:10], unit, 1.0 / QMAX, ALU.mult, ALU.mult))
                    step(dve.tensor_scalar(col[:, to:to + 1], col[:, 13:14], 1e-12, None, ALU.max))
                    step(dve.reciprocal(col[:, 13:14], col[:, to:to + 1]))
                    step(dve.tensor_scalar(col[:, 11:12], col[:, 13:14], unit, None, ALU.mult))

            def quantize(t, done=None):
                step(dve.tensor_scalar(t, t, col[:, 11:12], MAGIC, ALU.mult, ALU.add))
                last = dve.tensor_scalar(t, t, MAGIC + QMAX, -MAGIC, ALU.min, ALU.add)
                if done is None:
                    step(last)
                else:
                    last.then_inc(done, 1)

            dve.wait_ge(ln[2]["norm"], 1)
            scale_of(XN[:], 10)
            quantize(XN[:], ln[2]["norm"])
            dve.wait_ge(s["up_copied"], 3)
            scale_of(UP, 12)
            quantize(UP)
            for t in range(3):
                dve.wait_ge(s["gate_ready"], t + 1)
                b = 2 * ((t + 3) % 4)
                step(dve.tensor_scalar(GA[:, t, :], ps[:, b:b + 2, :].rearrange("p b n -> p (b n)"), col[:, 10:11], None, ALU.mult))
            scale_of(GA, 14)
            quantize(GA, s["gate_copied"])
            dve.wait_ge(s["sig_done"], 1)
            step(dve.tensor_scalar(FB, FB, 65536.0, MAGIC, ALU.mult, ALU.add))
            step(dve.tensor_scalar(FB, FB, MAGIC + 65535.0, -MAGIC, ALU.min, ALU.add))
            step(dve.tensor_scalar(col[:, 17:18], col[:, 14:15], 1.0 / 65536.0, None, ALU.mult))
            step(dve.scalar_tensor_tensor(GA, GA, col[:, 17:18], FB, ALU.mult, ALU.mult))
            scale_of(GA, 15)
            quantize(GA)
            step(dve.tensor_tensor(GA, GA, UP, ALU.mult))
            step(dve.tensor_scalar(col[:, 18:19], col[:, 15:16], col[:, 12:13], None, ALU.mult))
            scale_of(GA, 16, unit=col[:, 18:19])
            quantize(GA, s["oq_ready"])
            for half in range(2):
                dve.wait_ge(s["y_ready"], half + 1)
                xs = slice(4 * half, 4 * half + 4)
                dve.scalar_tensor_tensor(XN[:, xs, :], ps[:, half, :].rearrange("p (t d) -> p t d", t=4), col[:, 16:17],
                                         X[:, xs, :], ALU.mult, ALU.add).then_inc(s["y_done"], 1)

        @block.tensor
        def _(pe):
            mm = pe.matmul

            def norm_t(k, count=1):
                pe.wait_ge(ln[k]["norm"], count)
                for t in range(NT):
                    last = pe.transpose(ps[:, t // 4, (t % 4) * P:(t % 4) * P + P], XN[:, t, :], ident[:])
                    if t % 4 == 3:
                        last.then_inc(ln[k]["T"], 1)

            pe.wait_ge(s["consts"], 16)
            norm_t(0)
            pe.wait_ge(s["weights_loaded"], 192)
            for half in range(2):
                pe.wait_ge(ln[0]["copied"], half + 1)
                xt = XT[:, half * 512:half * 512 + 512]
                mm(ps[0:DC, 4 + half, :], w_dkv[:], xt, start=True, stop=True).then_inc(s["lat_ready"], 1)
                mm(ps[0:DC, 2 + half, :], w_dq[:], xt, start=True, stop=True).then_inc(s["lat_ready"], 1)
            pe.wait_ge(s["lat_copied"], 3)
            for half in range(2):
                last = mm(ps[:, 2 + half, :], w_uk[:], lat[:, 1, half * 512:half * 512 + 512], start=True, stop=True)
            last.then_inc(s["qk_ready"], 1)
            for half in range(2):
                last = mm(ps[:, half, :], w_uq[:], lat[:, 0, half * 512:half * 512 + 512], start=True, stop=True)
            last.then_inc(s["qk_ready"], 1)
            for t in range(NT):
                last = mm(ps[:, 6 + t // 4, (t % 4) * P:(t % 4) * P + P], lat[:, 1, t * P:t * P + P], w_uv[:], start=True, stop=True)
                if t % 4 == 3:
                    last.then_inc(s["vs_ready"], 1)

            def chunk_step(k, c, b, n, tiles):
                if k in (0, 1):
                    if k == 0:
                        pe.wait_ge(s["ctxT_ready"], c + GRANT)
                    mine = tiles[2 * k:2 * k + 2]
                    for t, m in mine:
                        last = pe.transpose(ps[:, 4, t * P:t * P + m], C[0:m, b, t, :], ident[0:m, 0:m])
                    if k == 1:
                        last.then_inc(s["ctx_t_ready"], 1)
                elif k == 2:
                    pe.wait_ge(s["ctxT_ready"], c + (1 + GRANT))
                    pe.wait_ge(s["k_copied"], c + GRANT)
                    mm(ps[:, 5, 0:n], w_k[:], CT[:, b, 0:n], start=True, stop=True).then_inc(s["k_ready"], 1)
                elif k < 7:
                    if k == 3:
                        pe.wait_ge(s["v_copied"], c + GRANT)
                    if k - 3 < len(tiles):
                        t, m = tiles[k - 3]
                        last = mm(ps[0:m, 6, t * P:t * P + P], CT[:, b, t * P:t * P + m], w_v[:], start=True, stop=True)
                        if t == len(tiles) - 1:
                            last.then_inc(s["v_ready"], 1)
                else:
                    pe.wait_ge(s["k_sq"], c + 1)
                    pe.wait_ge(s["n_copied"], c + GRANT)
                    mm(ps[:, 7, 0:n], headsum[:], csq[:, 0:n], start=True, stop=True).then_inc(s["n_ready"], 1)

            def max_unit(i, v):
                slot, qt = v // NT, v % NT
                r = 2 * (v % 2)
                pe.wait_ge(s["m_reduced"], i * (2 * NT) + (v + 1))
                if isinstance(i, int):
                    lhs, rhs = QQ[0:ROWS, 2 * i + slot, qt * P:qt * P + P], KS[:, i, :]
                else:
                    lhs = QQ[0:ROWS, bass.ds(i * 2 + slot, 1), qt * P:qt * P + P].rearrange("r o q -> r (o q)")
                    rhs = KS[:, bass.ds(i, 1), :].rearrange("r o k -> r (o k)")
                n = (qt + 1) * P
                for b in range((n + 511) // 512):
                    lo, hi = 512 * b, min(n, 512 * b + 512)
                    mm(ps[:, r + b, 0:hi - lo], lhs, rhs[:, lo:hi], start=True, stop=hi < n)
                mm(ps[:, r + b, n - P - lo:n - lo], identb[:], mask[:, 1, :], start=False, stop=True).then_inc(s["m_scores"], 1)

            pe.wait_ge(s["q_spread"], 192)
            pe.wait_ge(s["ks_spread"], 96)
            pe.wait_ge(s["vs_copied"], NT)
            pe.wait_ge(s["identb_ready"], 1)
            whole = [(t, P) for t in range(CH)]
            with pe.Fori(0, NCH // 2) as i:
                for v in range(2 * NT):
                    max_unit(i, v)
                    if v % 8 == 0:
                        pe.wait_ge(ctx_loaded[v // 8], 16 * i + 16)
                    chunk_step(v % 8, 2 * i + v // 8, v // 8, CH * P, whole)
            pe.wait_ge(s["ctx_tail_loaded"], 32)
            for v in range(2 * NT):
                max_unit(NCH // 2, v)
                if v < 8:
                    chunk_step(v, NCH, 0, REST, [(0, P), (1, P), (2, TAIL)])
            pe.wait_ge(s["w_ready"], 1)
            pe.wait_ge(s["v_copied"], NCH + 1 + GRANT)
            for v in range(2 * NT):
                max_unit(NCH // 2 + 1, v)
                if v < 9:
                    last = pe.transpose(ps[:, 4 + v // 3, (v % 3) * P:(v % 3) * P + P], wraw[:, v, :], ident[:])
                    if v % 3 == 2:
                        last.then_inc(s["w_t_ready"], 1)

            def negs(parts, count, done):
                pe.wait_ge(parts, count)
                for k in range(3):
                    last = pe.transpose(ps[:, 0, :].bitcast(bf16)[:, k * P:k * P + P], npart[:, k, :], identb[:])
                last.then_inc(done, 1)

            negs(s["neg_parts"], 1, s["neg_t"])
            pe.wait_ge(s["neg_rows"], 48)
            pe.wait_ge(s["w_t_copied"], 3)
            pe.wait_ge(s["n_copied"], NCH + 2 + GRANT)

            def self_scores(u, qb, kt, p):
                if u >= 3:
                    pe.wait_ge(s["self_exp"], u - 2)
                lo = first_query(qb, kt)
                diag = kt >= 4 * qb
                for a in range(2):
                    bank = ps[:, 2 * (u % 3) + a, :]
                    last = mm(bank[:, lo:HALF], KS[:, p, kt * P:kt * P + P], QQ[0:ROWS, 2 * p + a, qb * HALF + lo:qb * HALF + HALF],
                              start=True, stop=not diag)
                    if diag:
                        last = mm(bank[:, lo:lo + P], identb[:], mask[:, 0, :], start=False, stop=True)
                last.then_inc(s["self_ready"], 1)

            def window(v, h):
                c, j = h % 4, h // 4
                flat = v[:, c].rearrange("p j e -> p (j e)")
                return flat[:, 23 * j:23 * j + 32] if j < 3 else flat[:, 96:128]

            def four_heads(v, pair, lo, start, stop):
                for h in range(2 * pair, 2 * pair + 4):
                    c, j = h % 4, h // 4
                    last = mm(ps[32 * c:32 * c + 32, 6 + j // 3, lo:HALF], window(v, h), PR[:, h // 2, h % 2, lo:HALF],
                              start=start and j in (0, 3), stop=stop and j in (2, 3))
                return last

            units = self_units()
            LAG = 2
            groups = len(units) // 2
            for g in range(groups + LAG):
                if g < groups:
                    for u in (2 * g, 2 * g + 1):
                        self_scores(u, *units[u])
                if g >= LAG:
                    qb, kt, p = units[2 * (g - LAG)]
                    if (qb, kt, p) == (1, 0, 0):
                        pe.wait_ge(s["self_out"], 1)
                    pe.wait_ge(s["self_exp"], 2 * (g - LAG) + 2)
                    four_heads(VS[:, kt], p, first_query(qb, kt), kt == 0, kt == 4 * qb + 3).then_inc(s["self_pv"], 1)

            def finish(k, out_ready, w):
                pe.wait_ge(out_ready, 2)
                for a in range(2):
                    for t in range(NT):
                        last = pe.transpose(ps[:, 2 * a + t // 4, (t % 4) * P:(t % 4) * P + P], OT[:, a, t * P:t * P + P], ident[:])
                last.then_inc(fin[k]["back"], 1)
                pe.wait_ge(fin[k]["attn"], 1)
                for t in range(NT):
                    last = pe.transpose(ps[:, t // 4, (t % 4) * P:(t % 4) * P + P], XN[:, t, :], ident[:])
                    if t % 4 == 3:
                        last.then_inc(fin[k]["attnT"], 1)
                for t in range(NT):
                    pe.wait_ge(fin[k]["attnTc"], t // 4 + 1)
                    last = mm(ps[:, 2 + t // 4, (t % 4) * P:(t % 4) * P + P], XT[:, t * P:t * P + P], w[:], start=True, stop=True)
                last.then_inc(fin[k]["y"], 1)

            finish(0, s["self_out"], w_os)
            norm_t(1)
            for half in range(2):
                pe.wait_ge(ln[1]["copied"], half + 1)
                last = mm(ps[:, 4 + half, :], w_q[:], XT[:, half * 512:half * 512 + 512], start=True, stop=True)
            last.then_inc(s["xq_ready"], 1)
            pe.wait_ge(s["xsq"], 1)
            for half in range(2):
                last = mm(ps[:, 6 + half, :], headsum[:], kpart[:, 0, half * 512:half * 512 + 512], start=True, stop=True)
            last.then_inc(s["x_norm"], 1)
            pe.wait_ge(s["xq_spread"], 192)
            pe.wait_ge(s["q_cleared"], 1)
            pe.wait_ge(s["flag_ready"], 1)
            pe.wait_ge(kx_loaded[0], 96)
            exact = pe.value_load(flag[0:1, 0:1], min_val=0, max_val=1)
            with pe.If(exact > 0):
                def scan(t, n, loaded):
                    with pe.Fori(0, NP) as i:
                        if loaded is not None:
                            pe.wait_ge(s["slow_loaded"], loaded)
                        for sl in range(2):
                            v = t * H + i * 2
                            pe.wait_ge(s["slow_reduced"], (v + sl) * 2 + 1)
                            for qt in range(NT):
                                last = mm(ps[:, 2 * sl + qt // 4, (qt % 4) * P:(qt % 4) * P + n],
                                          QQ[0:ROWS, bass.ds(i * 2 + sl, 1), qt * P:qt * P + P].rearrange("r o q -> r (o q)"),
                                          KX[:, 0, bass.ds(i, 1), 0:n].rearrange("r o k -> r (o k)"), start=True, stop=True)
                            last.then_inc(s["slow_scores"], 1)

                scan(0, P, None)
                with pe.Fori(1, KT - 1) as t:
                    scan(t, P, t * (16 * TERMS))
                scan(KT - 1, TAIL, (KT - 1) * (16 * TERMS))
                negs(s["slow_neg"], 4, s["slow_t"])
                pe.wait_ge(s["slow_loaded"], KT * (16 * TERMS))
                pe.wait_ge(s["slow_rows"], 48)

            LOAD = 16 * TERMS

            def clear():
                for bank in (6, 7):
                    mm(ps[:, bank, :], zeros[0:ROWS, :], QQ[0:ROWS, 0, 0:HALF], start=True, stop=False)

            def close():
                for bank in (6, 7):
                    last = mm(ps[:, bank, :], zeros[0:ROWS, :], QQ[0:ROWS, 0, 0:HALF], start=False, stop=True)
                return last

            def cross_tile(qb, units_before, tiles_before, r, loaded, first=False):
                pe.wait_ge(kx_loaded[r], loaded)
                for p in range(UNITS):
                    if not (first and qb == 0 and p < 3):
                        pe.wait_ge(s["x_exp"], units_before + (p - 2))
                    b = 2 * ((UNITS * r + p) % 3)
                    for a in range(2):
                        last = mm(ps[:, b + a, :], KX[:, r, p, :], QQ[0:ROWS, 2 * p + a, qb * HALF:qb * HALF + HALF],
                                  start=True, stop=True)
                    last.then_inc(s["xs_ready"], 1)
                    if p % 2 == 0 or (first and qb == 0 and p < 5):
                        continue
                    if p == 5:
                        pe.wait_ge(s["v_staged"], tiles_before + 1)
                        if first:
                            if qb:
                                pe.wait_ge(s["x_out"], 1)
                            clear()
                    pe.wait_ge(s["x_exp"], units_before + (p - 3))
                    last = four_heads(VX[:, r if p > 3 else (r - 1) % 3], (p - 5) % UNITS, 0, False, False)
                    if first and p == 3:
                        last = close()
                    last.then_inc(s["x_pv"], 1)

            for qb in range(2):
                for r in range(3):
                    t = qb * KT + r
                    cross_tile(qb, UNITS * t, t, r, LOAD * (KT // 3 * qb + 1), first=r == 0)
                with pe.Fori(1, KT // 3) as i:
                    for r in range(3):
                        cross_tile(qb, i * (3 * UNITS) + UNITS * (qb * KT + r), i * 3 + (qb * KT + r), r,
                                   i * LOAD + LOAD * (KT // 3 * qb + 1))
            pe.wait_ge(s["x_exp"], 2 * KT * UNITS)
            four_heads(VX[:, (KT - 1) % 3], UNITS - 4, 0, False, False).then_inc(s["x_pv"], 1)
            four_heads(VX[:, (KT - 1) % 3], UNITS - 2, 0, False, False)
            close().then_inc(s["x_pv"], 1)
            finish(1, s["x_out"], w_ox)

            norm_t(2, count=2)
            pe.wait_ge(ln[2]["copied"], 2)
            for t in range(3):
                for g in range(2):
                    last = mm(ps[:, 2 * t + g, :], wT[:, 3 + t, :], XT[:, 512 * g:512 * g + 512], start=True, stop=True)
                last.then_inc(s["up_ready"], 1)
            for t in range(3):
                if t:
                    pe.wait_ge(s["up_copied"], t)
                for g in range(2):
                    last = mm(ps[:, 2 * ((t + 3) % 4) + g, :], wT[:, t, :], XT[:, 512 * g:512 * g + 512], start=True, stop=True)
                last.then_inc(s["gate_ready"], 1)
            pe.wait_ge(s["oq_ready"], 1)
            for t in range(NT):
                for k in range(3):
                    last = mm(ps[:, t // 4, (t % 4) * P:(t % 4) * P + P], GA[:, k, t * P:t * P + P], wT[:, 6 + k, :],
                              start=k == 0, stop=k == 2)
                if t % 4 == 3:
                    last.then_inc(s["y_ready"], 1)


_INS = ['x', 'ctx_1024', 'L0_attn_W_dq', 'L0_attn_W_uq', 'L0_attn_W_dkv', 'L0_attn_W_uk', 'L0_attn_W_uv', 'L0_attn_W_o',
        'L0_xattn_Wq', 'L0_xattn_Wk', 'L0_xattn_Wv', 'L0_xattn_Wo', 'L0_ffn_w_gate', 'L0_ffn_w_up', 'L0_ffn_w_down']


def kernel(**inputs):
    import ml_dtypes
    import concourse.bacc as _bacc
    from concourse.bass_utils import run_bass_kernel_spmd as _run

    nc = _bacc.Bacc("TRN2", target_bir_lowering=False, num_devices=1)
    at = np.arange(P)
    masks = np.zeros((P, 2, P), np.float32)
    masks[:, 0, :] = np.where(at[:, None] > at[None, :], MASKED, 0.0)
    masks[:, 1, :] = np.where(at[None, :] > at[:, None], MASKED, 0.0)
    heads = (at[:, None] // DK == at[None, :] // DK)
    arrays, args = {}, []
    for name in _INS:
        a = np.ascontiguousarray(inputs[name])
        arrays[f"in_{name}"] = a
        args.append(nc.dram_tensor(f"in_{name}", a.shape, mybir.dt.from_np(a.dtype), kind="ExternalInput").ap())
    for name, a in (("ident", np.eye(P, dtype=np.float32)), ("masks", masks.astype(ml_dtypes.bfloat16)),
                    ("heads", heads.astype(ml_dtypes.bfloat16))):
        arrays[f"const_{name}"] = a
        args.append(nc.dram_tensor(f"const_{name}", a.shape, mybir.dt.from_np(a.dtype), kind="ExternalInput").ap())
    args.append(nc.dram_tensor("out", (1, S, D), mybir.dt.float32, kind="ExternalOutput").ap())
    build(nc, *args)
    r = _run(nc, [arrays], core_ids=[0])
    return r.results[0]["out"]
```

```python
from contextlib import ExitStack

import numpy as np

import concourse.bass as bass
from concourse import mybir

S, SC, D, H, DK, DC, FF = 1024, 6404, 128, 16, 8, 32, 384
P = 128
NT = S // P
NP = H // 2
KT = SC // P + 1
TAIL = SC - (KT - 1) * P
CH = 4
NCH = KT // CH
REST = SC - NCH * CH * P
KPART = (0, 1, 2, 0, 1, 0)
QPART = (0, 0, 0, 1, 1, 2)
KRUNS = ((0, 3), (3, 2), (5, 1))
KLOAD = 16 * len(KRUNS)
TERMS = len(KPART)
SHIFT, SELF_ROWS, ROWS = 96, 99, 100
TWO_ONES = float(np.uint32(0x3F803F80).view(np.float32))
BLOCKS = 24
HALF = 512
UNITS = NP
BLK = 32
QMAX, WMAX = 32767.0, 7.0
MAGIC = 1.5 * 2.0 ** 23
MASKED = -1.0e38
SAFE = 40.0
EPS = 1e-5


def build(nc, x, ctx, wdq, wuq, wdkv, wuk, wuv, wo_s, wq, wk, wv, wo_x, wg, wu, wd,
          ident_in, mask_in, heads_in, out, force_exact=False):
    f32, bf16, i32 = mybir.dt.float32, mybir.dt.bfloat16, mybir.dt.int32
    ALU, ACT, AX = mybir.AluOpType, mybir.ActivationFunctionType, mybir.AxisListType
    ABSMAX = bass.bass_isa.ReduceOp.absmax

    st = ExitStack()
    with st:
        def sb(name, shape, dt=f32):
            return st.enter_context(nc.sbuf_tensor(name, shape, dt))

        def sem(name):
            return st.enter_context(nc.semaphore(name))

        q_dram = nc.dram_tensor("q_parts", (2, 3, P, S), bf16, kind="Internal").ap()
        ks_dram = nc.dram_tensor("self_k_parts", (3, P, S), bf16, kind="Internal").ap()
        kx_dram = nc.dram_tensor("ctx_k_parts", (3, P, KT * P), bf16, kind="Internal").ap()

        ident = sb("ident", [P, P])
        identb = sb("identb", [P, P], bf16)
        mask = sb("mask", [P, 2, P], bf16)
        headsum = sb("headsum", [P, P], bf16)
        zeros = sb("zeros", [P, P], bf16)
        eps = sb("eps", [P, 1])
        w_dq = sb("w_dq", [D, DC])
        w_uq = sb("w_uq", [DC, D])
        w_dkv = sb("w_dkv", [D, DC])
        w_uk = sb("w_uk", [DC, D])
        w_uv = sb("w_uv", [DC, D])
        w_os = sb("w_os", [D, D])
        w_q = sb("w_q", [D, D])
        w_k = sb("w_k", [D, D])
        w_v = sb("w_v", [D, D])
        w_ox = sb("w_ox", [D, D])
        wraw = sb("wraw", [P, 9, P])
        wmax = sb("wmax", [P, 36])
        wscale = sb("wscale", [P, 36])
        wT = sb("wT", [P, 9, P])

        X = sb("X", [P, NT, D])
        XN = sb("XN", [P, NT, D])
        XT = sb("XT", [D, S])
        stats = sb("stats", [P, NT, 6])
        moments = sb("moments", [P, NT, 2])
        std = sb("std", [P, NT])
        rstd = sb("rstd", [P, NT])
        part = sb("part", [P, 3, S], bf16)
        kpart = sb("kpart", [P, 3, S], bf16)
        QQ = sb("QQ", [P, H, S], bf16)
        KS = sb("KS", [ROWS, NP, S], bf16)
        KX = sb("KX", [ROWS, 3, NP, P], bf16)
        VS = sb("VS", [P, NT, 4, 4, 32])
        V9 = sb("V9", [P, KT, H, 9])
        VX = sb("VX", [P, 3, 4, 4, 32])
        PR = sb("PR", [P, 8, 2, HALF])
        OT = sb("OT", [P, 2, S])
        rec = sb("rec", [P, 2, 2, NT * 2, 2])
        mx = sb("mx", [P, H * NT])
        mhigh = sb("mhigh", [P, H, NT // 2])
        mtmp = sb("mtmp", [P, NT])
        ksn = sb("ksn", [P, HALF], bf16)
        ksmax = sb("ksmax", [P, HALF], bf16)
        npart = sb("npart", [P, 3, H * NT], bf16)
        nrem = sb("nrem", [P, H * NT])
        nT = sb("nT", [H * NT // 2, 2, 3, P], bf16)
        C = sb("C", [P, 2, CH, D])
        CT = sb("CT", [D, 2, CH * P])
        cpart = sb("cpart", [P, 2, 3, CH * P], bf16)
        col = sb("col", [P, 24])
        flag = sb("flag", [1, 1], i32)
        ps = st.enter_context(nc.psum_tensor("ps", [P, 8, HALF], f32))

        prf = PR[:].rearrange("p u a n -> p u (a n)")
        lat = prf[0:DC, 0:2, :]
        crem, kf = prf[:, 2, 0:HALF], prf[:, 3, 0:HALF]
        csq = prf[:, 2, HALF:S].bitcast(bf16)[:, 0:HALF]
        rem = OT[:, 0, :]
        UP, GA = prf[:, 0:3, :], prf[:, 3:6, :]
        FB = QQ[:, 0:6, :].bitcast(f32).rearrange("p (t a) s -> p t (a s)", t=3)
        wb = wraw[:].rearrange("p t (b i) -> p (t b) i", i=BLK)
        sc, winv = (w[:].rearrange("p (b o) -> p b o", o=1).to_broadcast([P, 36, BLK]) for w in (wscale, wmax))

        names = """consts x_loaded weights_loaded ffn_w_loaded ctx_tail_loaded identb_ready
            n_used ctx_t_ready ctxT_ready k_ready k_copied k_rem k_part2 k_sq k_parts k_tail_stored v_ready v_copied n_ready n_copied
            w_ready w_t_ready w_t_copied pool_step pool_init dve_step q_stored ks_stored
            lat_ready lat_copied qk_ready qk_first qk_parts vs_ready vs_copied m_scores m_reduced neg_parts neg_t neg_copied
            neg_rows self_ready self_exp self_pv self_out q_cleared xq_ready xq_first xq_parts xsq x_norm xq_stored
            bound_col bound_all bound_root flag_ready slow_loaded slow_scores slow_reduced slow_neg slow_t slow_copied
            slow_rows xs_ready x_exp x_pv x_out v_staged am_col am_all up_ready up_copied gate_ready gate_copied gate_q sig_raw sig_done
            oq_ready y_ready y_done out_stored""".split()
        s = {n: sem(n) for n in names}
        ctx_loaded = [sem(f"ctx_loaded{b}") for b in range(2)]
        kx_loaded = [sem(f"kx_loaded{b}") for b in range(3)]
        k_stored = sem("k_stored")
        q_spread, ks_spread = ([sem(f"{n}{h}") for h in range(2)] for n in ("q_spread", "ks_spread"))
        xq_spread = [sem(f"xq_spread{h}") for h in range(2)]
        ln = [{n: sem(f"ln{k}_{n}") for n in ("var", "std", "norm", "T", "copied")} for k in range(3)]
        fin = [{n: sem(f"fin{k}_{n}") for n in ("back", "attn", "attnT", "attnTc", "y", "res")} for k in range(2)]
        granted = ("ctxT_ready", "k_sq", "k_copied", "k_rem", "v_copied", "n_copied")
        GRANT = 1

        def fill_keys(eng, dst, src, done, pairs=slice(0, NP)):
            for lo, n in KRUNS:
                eng.dma_start(dst[lo * 16:(lo + n) * 16, pairs], src[0:n].rearrange("i (r p) n -> (i r) p n", r=16)[:, pairs]).then_inc(done, 16)

        def fill_queries(eng, k, done, at, pairs=slice(0, NP)):
            for i, part_no in enumerate(QPART):
                for slot in range(2):
                    r = i * 16 + slot * 8
                    eng.dma_start(QQ[r:r + 8, 2 * pairs.start + slot:2 * pairs.stop:2, at],
                                  q_dram[k, part_no].rearrange("(s d p) n -> s d p n", s=2, d=DK)[slot, :, pairs, at]).then_inc(done, 16)

        def fill_shift(eng, hh, done):
            for i in range(3):
                eng.dma_start(QQ[SHIFT + i:SHIFT + i + 1, NP * hh:NP * hh + NP, :].rearrange("o h (t q) -> o (h t) q", q=P),
                              nT[:, hh, i, :]).then_inc(done, 16)

        def self_units():
            return [(hh, qb, kt, 4 * hh + p) for hh in range(2) for qb in range(2) for kt in range(4 * qb + 4) for p in range(4)]

        def max_blocks():
            order = (7, 15, 3, 6, 5, 4, 14, 2, 1, 13, 0, 12)
            return [(slot, v % NT, v // NT, min(HALF, (v % NT + 1) * P - HALF * (v // NT))) for slot in range(2) for v in order]

        EARLY = BLOCKS // 3

        def self_bank(u):
            return 4 if u < EARLY else 2 * (u % 3)

        def first_query(qb, kt):
            return max(0, kt * P - qb * HALF)

        block = st.enter_context(nc.Block())

        @block.sync
        def _(sp):
            def load_chunk(c, b):
                src = ctx[0, 0:NCH * CH * P, :].rearrange("(c t p) d -> c p t d", p=P, t=CH)[bass.ds(c, 1)]
                sp.dma_start(C[:, b, :, :], src.rearrange("c p t d -> p (c t) d")).then_inc(ctx_loaded[b], 16)

            sp.dma_start(X[:], x[0].rearrange("(t p) d -> p t d", p=P)).then_inc(s["x_loaded"], 16)
            sp.dma_start(ident[:], ident_in).then_inc(s["consts"], 16)
            for dst, src in ((w_dq, wdq), (w_dkv, wdkv), (w_uq, wuq), (w_uk, wuk), (w_uv, wuv)):
                sp.dma_start(dst[:], src).then_inc(s["weights_loaded"], 16)
            sp.dma_start(mask[:], mask_in).then_inc(s["weights_loaded"], 16)
            for k, w in enumerate((wg, wu)):
                sp.dma_start(wraw[:, 3 * k:3 * k + 3, :], w.rearrange("(t p) i -> p t i", p=P)).then_inc(s["ffn_w_loaded"], 16)
            sp.dma_start(wraw[:, 6:9, :], wd.rearrange("o (t i) -> o t i", i=P)).then_inc(s["ffn_w_loaded"], 16)
            for dst, src in ((w_k, wk), (w_v, wv.rearrange("d n h -> d (n h)")), (w_q, wq)):
                sp.dma_start(dst[:], src).then_inc(s["weights_loaded"], 16)
            sp.dma_start(headsum[:], heads_in).then_inc(s["weights_loaded"], 16)
            sp.dma_start(w_ox[:], wo_x.rearrange("n h d -> (n h) d")).then_inc(s["weights_loaded"], 16)
            sp.dma_start(w_os[:], wo_s).then_inc(s["weights_loaded"], 16)
            for b in range(2):
                load_chunk(b, b)

            sp.wait_ge(s["qk_parts"], 1)
            sp.dma_start(q_dram[0].rearrange("i p n -> p i n"), part[:]).then_inc(s["q_stored"], 16)
            sp.wait_ge(s["qk_parts"], 2)
            sp.dma_start(ks_dram.rearrange("i p n -> p i n"), kpart[:]).then_inc(s["ks_stored"], 16)
            sp.wait_ge(s["pool_init"], 1)
            sp.wait_ge(s["q_stored"], 16)
            first, second = slice(0, NP // 2), slice(NP // 2, NP)
            fill_queries(sp, 0, q_spread[0], slice(0, S), first)
            sp.wait_ge(s["ks_stored"], 16)
            fill_keys(sp, KS[:], ks_dram, ks_spread[0], first)
            fill_queries(sp, 0, q_spread[1], slice(0, S), second)
            fill_keys(sp, KS[:], ks_dram, ks_spread[1], second)

            with sp.Fori(1, NCH // 2) as i:
                for b in range(2):
                    sp.wait_ge(s["ctx_t_ready"], 2 * i + (b - 1))
                    load_chunk(2 * i + b, b)
            sp.wait_ge(s["ctx_t_ready"], NCH - 1)
            lo = NCH * CH * P
            sp.dma_start(C[:, 0, 0:2, :], ctx[0, lo:lo + 2 * P, :].rearrange("(t p) d -> p t d", p=P)).then_inc(s["ctx_tail_loaded"], 16)
            sp.dma_start(C[0:TAIL, 0, 2, :], ctx[0, lo + 2 * P:SC, :]).then_inc(s["ctx_tail_loaded"], 16)
            for hh in range(2):
                sp.wait_ge(s["neg_copied"], hh + 1)
                fill_shift(sp, hh, s["neg_rows"])

            def load_keys(t, n, b, done):
                fill_keys(sp, KX[:, b, :, 0:n], kx_dram[:, :, bass.ds(t * P, n)], done)

            sp.wait_ge(k_stored, 16 * NCH)
            sp.wait_ge(s["k_tail_stored"], 16)
            for t in range(3):
                load_keys(t, P, t, kx_loaded[t])
            for h in range(2):
                at = slice(h * HALF, h * HALF + HALF)
                sp.wait_ge(s["xq_parts"], h + 1)
                sp.dma_start(q_dram[1].rearrange("i p n -> p i n")[:, :, at], part[:, :, at]).then_inc(s["xq_stored"], 16)
                sp.wait_ge(s["xq_stored"], 16 * h + 16)
                fill_queries(sp, 1, xq_spread[h], at)

            sp.wait_ge(s["flag_ready"], 1)
            exact = sp.value_load(flag[0:1, 0:1], min_val=0, max_val=1)
            with sp.If(exact > 0):
                with sp.Fori(1, KT - 1) as t:
                    sp.wait_ge(s["slow_scores"], t * H)
                    load_keys(t, P, 0, s["slow_loaded"])
                sp.wait_ge(s["slow_scores"], (KT - 1) * H)
                load_keys(KT - 1, TAIL, 0, s["slow_loaded"])
                sp.wait_ge(s["slow_scores"], KT * H)
                load_keys(0, P, 0, s["slow_loaded"])
                sp.wait_ge(s["slow_copied"], 1)
                for hh in range(2):
                    fill_shift(sp, hh, s["slow_rows"])

            def reload_keys(step, t, n, b):
                sp.wait_ge(s["xs_ready"], step * UNITS - 2 * UNITS)
                load_keys(t, n, b, kx_loaded[b])

            for qb in range(2):
                if qb:
                    for t in range(3):
                        reload_keys(KT + t, t, P, t)
                with sp.Fori(1, KT // 3 - 1) as i:
                    for r in range(3):
                        reload_keys(3 * i + (qb * KT + r), 3 * i + r, P, r)
                for t in range(KT - 3, KT):
                    reload_keys(qb * KT + t, t, P if t < KT - 1 else TAIL, t % 3)
            ov = out[0].rearrange("(t p) d -> p t d", p=P)
            for half in range(2):
                sp.wait_ge(s["y_done"], half + 1)
                sp.dma_start(ov[:, 4 * half:4 * half + 4, :], XN[:, 4 * half:4 * half + 4, :]).then_inc(s["out_stored"], 16)
            sp.wait_ge(s["out_stored"], 32)

        @block.gpsimd
        def _(pool):
            steps = [0]

            def step(ins):
                steps[0] += 1
                ins.then_inc(s["pool_step"], 1)
                pool.wait_ge(s["pool_step"], steps[0])

            step(pool.memset(eps[:], EPS))
            step(pool.memset(ksn[:], 0.0))
            step(pool.memset(ksmax[:], 0.0))
            for n in granted:
                pool.memset(zeros[:], 0.0).then_inc(s[n], GRANT)
                pool.wait_ge(s[n], GRANT)
            pool.memset(zeros[:], 0.0).then_inc(s["m_reduced"], 4)
            pool.wait_ge(s["m_reduced"], 4)
            step(pool.memset(QQ[SHIFT:ROWS, :, :].bitcast(f32), TWO_ONES))
            step(pool.memset(QQ[0:SELF_ROWS, :, :].bitcast(i32), 0))
            pool.memset(KS[SHIFT:SELF_ROWS].bitcast(f32), TWO_ONES).then_inc(s["pool_init"], 1)
            pool.wait_ge(s["pool_init"], 1)
            step(pool.memset(VS[:], 0.0))
            step(pool.memset(VS[:, :, :, :, 8:9], 1.0))
            step(pool.memset(V9[:, 0:KT - 1, :, 8:9], 1.0))
            step(pool.memset(V9[:, KT - 1, :, :], 0.0))
            step(pool.memset(V9[0:TAIL, KT - 1, :, 8:9], 1.0))
            step(pool.memset(VX[:], 0.0))
            step(pool.memset(KX[SHIFT:ROWS].bitcast(f32), TWO_ONES))

            kv = kx_dram.rearrange("i p n -> p i n")

            def key_parts(c, b, n, stored, count):
                pool.wait_ge(s["k_copied"], c + (1 + GRANT))
                pool.tensor_tensor(crem[:, 0:n], kf[:, 0:n], cpart[:, b, 0, 0:n], ALU.subtract).then_inc(s["k_rem"], 1)
                pool.wait_ge(s["k_part2"], c + 1)
                pool.tensor_tensor(cpart[:, b, 2, 0:n], crem[:, 0:n], cpart[:, b, 1, 0:n], ALU.subtract).then_inc(s["k_parts"], 1)
                pool.wait_ge(s["k_parts"], c + 1)
                pool.dma_start(kv[:, :, bass.ds(c * (CH * P), n)], cpart[:, b, :, 0:n]).then_inc(stored, 16)
                pool.wait_ge(stored, count)

            with pool.Fori(0, NCH // 2) as i:
                for b in range(2):
                    key_parts(2 * i + b, b, CH * P, k_stored, i * 32 + (16 * b + 16))
            key_parts(NCH, 0, REST, s["k_tail_stored"], 16)
            pool.wait_ge(s["self_ready"], len(self_units()))
            pool.memset(QQ[SHIFT:ROWS - 1, :, :].bitcast(i32), 0).then_inc(s["q_cleared"], 1)
            pool.wait_ge(s["q_cleared"], 1)
            pool.wait_ge(s["bound_col"], 1)
            pool.partition_all_reduce(col[:, 2:3], col[:, 1:2], P, ABSMAX).then_inc(s["bound_all"], 1)
            for k in range(5):
                pool.wait_ge(s["am_col"], k + 1)
                pool.partition_all_reduce(col[:, 9:10], col[:, 8:9], P, ABSMAX).then_inc(s["am_all"], 1)

        @block.scalar
        def _(act):
            def norm(k, copies=True):
                for h in range(2):
                    act.wait_ge(ln[k]["var"], h + 1)
                    at = slice(4 * h, 4 * h + 4)
                    act.activation(std[:, at], moments[:, at, 1:2].rearrange("p t o -> p (t o)"), ACT.Sqrt, bias=eps[:]).then_inc(ln[k]["std"], 1)
                if copies:
                    for half in range(2):
                        act.wait_ge(ln[k]["T"], half + 1)
                        act.activation(XT[:, half * 512:half * 512 + 512], ps[:, half, :], ACT.Copy).then_inc(ln[k]["copied"], 1)

            act.wait_ge(s["pool_step"], 1)
            norm(0)
            for half in range(2):
                act.wait_ge(s["lat_ready"], 2 * half + 1)
                act.activation(lat[:, 1, half * 512:half * 512 + 512], ps[0:DC, 4 + half, :], ACT.Copy).then_inc(s["lat_copied"], 1)
            act.wait_ge(s["qk_ready"], 1)
            act.activation(part[:, 0, :], ps[:, 0:2, :].rearrange("p b n -> p (b n)"), ACT.Copy, scale=DK ** -0.5).then_inc(s["qk_first"], 1)
            act.wait_ge(s["qk_ready"], 2)
            act.activation(kpart[:, 0, :], ps[:, 2:4, :].rearrange("p b n -> p (b n)"), ACT.Copy).then_inc(s["qk_first"], 1)
            act.wait_ge(s["pool_step"], 7)
            for t in range(NT):
                act.wait_ge(s["vs_ready"], t // 4 + 1)
                act.activation(VS[:, t, :, :, 0:8],
                               ps[:, 6 + t // 4, (t % 4) * P:(t % 4) * P + P].rearrange("p (j c d) -> p c j d", j=4, d=DK),
                               ACT.Copy).then_inc(s["vs_copied"], 1)

            def chunk(c, b, n, values):
                act.wait_ge(s["ctx_t_ready"], c + 1)
                act.activation(CT[:, b, 0:n], ps[:, 4, 0:n], ACT.Copy).then_inc(s["ctxT_ready"], 1)
                act.wait_ge(s["k_ready"], c + 1)
                act.wait_ge(s["k_rem"], c + GRANT)
                act.activation(kf[:, 0:n], ps[:, 5, 0:n], ACT.Copy)
                act.activation(cpart[:, b, 0, 0:n], ps[:, 5, 0:n], ACT.Copy).then_inc(s["k_copied"], 1)
                act.activation(csq[:, 0:n], ps[:, 5, 0:n], ACT.Square).then_inc(s["k_sq"], 1)
                act.wait_ge(s["k_rem"], c + (1 + GRANT))
                act.activation(cpart[:, b, 1, 0:n], crem[:, 0:n], ACT.Copy).then_inc(s["k_part2"], 1)
                act.wait_ge(s["v_ready"], c + 1)
                values()
                act.wait_ge(s["n_ready"], c + 1)
                act.wait_ge(s["n_used"], c + 1)
                act.activation(ksn[:, 0:n], ps[:, 7, 0:n], ACT.Copy).then_inc(s["n_copied"], 1)

            act.wait_ge(s["pool_step"], 10)
            with act.Fori(0, NCH // 2) as i:
                for b in range(2):
                    def values():
                        act.activation(V9[:, bass.ds((2 * i + b) * CH, CH), :, 0:8],
                                       ps[:, 6, :].rearrange("p (t h d) -> p t h d", t=CH, d=DK), ACT.Copy).then_inc(s["v_copied"], 1)
                    chunk(2 * i + b, b, CH * P, values)

            def last_values():
                act.activation(V9[:, KT - 3:KT - 1, :, 0:8],
                               ps[:, 6, 0:2 * P].rearrange("p (t h d) -> p t h d", t=2, d=DK), ACT.Copy)
                act.activation(V9[0:TAIL, KT - 1, :, 0:8], ps[0:TAIL, 6, 2 * P:3 * P].rearrange("p (h d) -> p h d", d=DK),
                               ACT.Copy).then_inc(s["v_copied"], 1)
            chunk(NCH, 0, REST, last_values)
            for g in range(3):
                act.wait_ge(s["w_t_ready"], g + 1)
                act.activation(wT[:, 3 * g:3 * g + 3, :], ps[:, 4 + g, 0:3 * P].rearrange("p (t i) -> p t i", i=P),
                               ACT.Copy).then_inc(s["w_t_copied"], 1)

            act.wait_ge(s["k_parts"], NCH + 1)
            for u, (hh, qb, kt, p) in enumerate(self_units()):
                lo = first_query(qb, kt)
                act.wait_ge(s["self_ready"], u + 1)
                if u % 2 == 0 and u >= 8:
                    act.wait_ge(s["self_pv"], u // 2 - 3)
                b = self_bank(u)
                act.activation(PR[:, u % 8, :, lo:HALF], ps[:, b:b + 2, lo:HALF], ACT.Exp).then_inc(s["self_exp"], 1)

            def finish(k):
                for half in range(2):
                    act.wait_ge(fin[k]["attnT"], half + 1)
                    act.activation(XT[:, half * 512:half * 512 + 512], ps[:, 2 * half, :], ACT.Copy).then_inc(fin[k]["attnTc"], 1)

            finish(0)
            norm(1)
            for h in range(2):
                at = slice(h * HALF, h * HALF + HALF)
                act.wait_ge(s["xq_ready"], h + 1)
                act.activation(part[:, 0, at], ps[:, 4 + h, :], ACT.Copy, scale=DK ** -0.5).then_inc(s["xq_first"], 1)
            act.wait_ge(s["bound_all"], 1)
            act.activation(col[:, 3:4], col[:, 2:3], ACT.Sqrt).then_inc(s["bound_root"], 1)

            def exp_tile(base, r, start=False):
                for p in range(UNITS):
                    act.wait_ge(s["xs_ready"], base + (p + 1))
                    if p % 2 == 0 and not start:
                        act.wait_ge(s["x_pv"], half_of(base) + (p // 2 - 3))
                    b = 2 * ((UNITS * r + p) % 3)
                    act.activation(PR[:, p, :, :], ps[:, b:b + 2, :], ACT.Exp).then_inc(s["x_exp"], 1)

            for qb in range(2):
                for r in range(3):
                    base = (qb * KT + r) * UNITS
                    half_of = lambda v: v // 2
                    exp_tile(base, r, start=base == 0)
                with act.Fori(1, KT // 3) as i:
                    for r in range(3):
                        half_of = lambda v: i * (3 * UNITS // 2) + (qb * KT + r) * UNITS // 2
                        exp_tile(i * (3 * UNITS) + (qb * KT + r) * UNITS, r)
            finish(1)
            norm(2, copies=False)
            for ready, dst, first, copied in ((s["up_ready"], UP, 0, s["up_copied"]), (s["gate_ready"], GA, 3, s["gate_copied"])):
                for t in range(3):
                    act.wait_ge(ready, t + 1)
                    b = 2 * ((t + first) % 4)
                    act.activation(dst[:, t, :], ps[:, b:b + 2, :].rearrange("p b n -> p (b n)"), ACT.Copy).then_inc(copied, 1)
            for t in range(3):
                act.wait_ge(s["gate_q"], t + 1)
                act.activation(FB[:, t, :], GA[:, t, :], ACT.Sigmoid, scale=col[:, 14:15]).then_inc(s["sig_raw"], 1)
                act.wait_ge(s["sig_raw"], t + 1)
                act.activation(FB[:, t, :], FB[:, t, :], ACT.Copy, scale=65536.0, bias=MAGIC).then_inc(s["sig_done"], 1)

        @block.vector
        def _(dve):
            steps = [0]

            def step(ins):
                steps[0] += 1
                ins.then_inc(s["dve_step"], 1)
                dve.wait_ge(s["dve_step"], steps[0])

            def norm_stats(k, h):
                for t in range(4 * h, 4 * h + 4):
                    last = dve.bn_stats(stats[:, t, :], X[:, t, :])
                step(last)
                for t in range(4 * h, 4 * h + 4):
                    last = dve.bn_aggr(moments[:, t, :], stats[:, t, :])
                last.then_inc(ln[k]["var"], 1)

            def norm_rows(k):
                for h in range(2):
                    dve.wait_ge(ln[k]["std"], h + 1)
                    step(dve.reciprocal(rstd[:, 4 * h:4 * h + 4], std[:, 4 * h:4 * h + 4]))
                    for t in range(4 * h, 4 * h + 4):
                        last = dve.tensor_scalar(XN[:, t, :], X[:, t, :], moments[:, t, 0:1], rstd[:, t:t + 1],
                                                 ALU.subtract, ALU.mult)
                    last.then_inc(ln[k]["norm"], 1)

            def mark(ins):
                steps[0] += 1
                ins.then_inc(s["dve_step"], 1)
                return steps[0]

            def after(count):
                dve.wait_ge(s["dve_step"], count)

            def rest(src, scale, dst, at=slice(0, S)):
                step(dve.scalar_tensor_tensor(rem[:, at], src, scale, dst[:, 0, at], ALU.mult, ALU.subtract))

            def other_parts(dst, done, at=slice(0, S)):
                step(dve.tensor_copy(dst[:, 1, at], rem[:, at]))
                dve.tensor_tensor(dst[:, 2, at], rem[:, at], dst[:, 1, at], ALU.subtract).then_inc(done, 1)

            dve.wait_ge(s["x_loaded"], 16)
            norm_stats(0, 0)
            norm_stats(0, 1)
            norm_rows(0)
            dve.wait_ge(s["consts"], 16)
            dve.tensor_copy(identb[:], ident[:]).then_inc(s["identb_ready"], 1)
            for half in range(2):
                dve.wait_ge(s["lat_ready"], 2 * half + 2)
                last = dve.tensor_copy(lat[:, 0, half * 512:half * 512 + 512], ps[0:DC, 2 + half, :])
            last.then_inc(s["lat_copied"], 1)
            dve.wait_ge(s["qk_first"], 1)
            rest(ps[:, 0:2, :].rearrange("p b n -> p (b n)"), DK ** -0.5, part[:])
            other_parts(part[:], s["qk_parts"])
            dve.wait_ge(s["qk_parts"], 1)
            dve.wait_ge(s["qk_first"], 2)
            rest(ps[:, 2:4, :].rearrange("p b n -> p (b n)"), 1.0, kpart[:])
            other_parts(kpart[:], s["qk_parts"])

            dve.wait_ge(s["ffn_w_loaded"], 48)
            step(dve.tensor_reduce(wmax[:], wb, AX.X, ALU.max, apply_absolute_value=True))
            step(dve.tensor_scalar(wscale[:], wmax[:], 1.0 / WMAX, 1e-12, ALU.mult, ALU.max))
            step(dve.reciprocal(wmax[:], wscale[:]))
            step(dve.tensor_tensor(wb, wb, winv, ALU.mult))
            step(dve.tensor_scalar(wraw[:], wraw[:], MAGIC, -MAGIC, ALU.add, ALU.add))
            step(dve.tensor_scalar(wraw[:], wraw[:], -WMAX - 1.0, WMAX, ALU.max, ALU.min))
            dve.tensor_tensor(wb, wb, sc, ALU.mult).then_inc(s["w_ready"], 1)

            def fold_norms(c, rows=HALF):
                dve.wait_ge(s["n_copied"], c + GRANT)
                dve.tensor_tensor(ksmax[:, 0:rows], ksmax[:, 0:rows], ksn[:, 0:rows], ALU.max).then_inc(s["n_used"], 1)

            def maxima(i, chunks):
                for v, (slot, qt, high, n) in enumerate(max_blocks()):
                    dve.wait_ge(s["m_scores"], i * BLOCKS + (v + 1))
                    dst = (mhigh[:, bass.ds(i * 2 + slot, 1), qt - 4:qt - 3].rearrange("p o t -> p (o t)") if high
                           else mx[:, bass.ds(i * (2 * NT) + (slot * NT + qt), 1)])
                    dve.reduce_max(dst, ps[:, v % 4, 0:n], AX.X).then_inc(s["m_reduced"], 1)
                    if v % (BLOCKS // 2) == BLOCKS // 2 - 2 and slot < chunks:
                        fold_norms(i * 2 + slot)

            def negatives(hh):
                dve.wait_ge(s["m_reduced"], (hh + 1) * (BLOCKS * NP // 2) + 4)
                at = slice(64 * hh, 64 * hh + 64)
                late = mx[:, at].rearrange("p (h t) -> p h t", t=NT)[:, :, 4:NT]
                step(dve.tensor_tensor(late, late, mhigh[:, NP * hh:NP * hh + NP, :], ALU.max))
                step(dve.tensor_scalar(npart[:, 0, at], mx[:, at], -1.0, None, ALU.mult))
                step(dve.scalar_tensor_tensor(nrem[:, at], mx[:, at], -1.0, npart[:, 0, at], ALU.mult, ALU.subtract))
                step(dve.tensor_copy(npart[:, 1, at], nrem[:, at]))
                dve.tensor_tensor(npart[:, 2, at], nrem[:, at], npart[:, 1, at], ALU.subtract).then_inc(s["neg_parts"], 1)
                dve.wait_ge(s["neg_t"], hh + 1)
                dve.tensor_copy(nT[:, hh].rearrange("p i q -> p (i q)"), ps[0:64, 7 * hh, :].bitcast(bf16)[:, 0:3 * P]).then_inc(s["neg_copied"], 1)

            with dve.Fori(0, NP // 2) as i:
                maxima(i, 2)
            negatives(0)
            with dve.Fori(NP // 2, NCH // 2) as i:
                maxima(i, 2)
            maxima(NCH // 2, 1)
            maxima(NCH // 2 + 1, 0)
            negatives(1)
            fold_norms(NCH + 1, REST)
            dve.wait_ge(s["n_used"], NCH + 2)
            step(dve.reduce_max(col[:, 0:1], ksmax[:], AX.X))

            def finish(k):
                for h in range(2):
                    dve.wait_ge(fin[k]["back"], h + 1)
                    tiles = slice(4 * h, 4 * h + 4)
                    two = ps[:, 2 * h:2 * h + 2, :].rearrange("p a (x r) -> p a x r", r=32)
                    step(dve.reciprocal(rec[:, h], two[:, :, :, 8:18:9]))
                    for j in range(4):
                        o = XN[:, tiles, j * 32:j * 32 + 32].rearrange("p t (c d) -> p t c d", c=4)
                        v = ps[:, 2 * h + j // 2, :].rearrange("p (t c r) -> p t c r", t=4, c=4)[:, :, :, 9 * (j % 2):9 * (j % 2) + 8]
                        f = rec[:, h, j // 2, :, j % 2:j % 2 + 1].rearrange("p (t c) o -> p t c o", t=4).to_broadcast([P, 4, 4, DK])
                        last = dve.tensor_tensor(o, v, f, ALU.mult)
                    last.then_inc(fin[k]["attn"], 1)
                for h in range(2):
                    dve.wait_ge(fin[k]["y"], h + 1)
                    rows = X[:, 4 * h:4 * h + 4, :].rearrange("p t d -> p (t d)")
                    dve.tensor_tensor(rows, rows, ps[:, 2 * h + 1, :], ALU.add).then_inc(fin[k]["res"], 1)
                    dve.wait_ge(fin[k]["res"], h + 1)
                    norm_stats(k + 1, h)
                norm_rows(k + 1)

            for n, (hh, qb, groups) in enumerate(((0, 0, 8), (0, 1, 24), (1, 0, 32), (1, 1, 48))):
                dve.wait_ge(s["self_pv"], groups)
                dve.tensor_copy(OT[:, hh, qb * HALF:qb * HALF + HALF], ps[:, 6 + qb, :]).then_inc(s["self_out"], 1)
            finish(0)
            halves = [slice(h * HALF, h * HALF + HALF) for h in range(2)]
            dve.wait_ge(s["xq_first"], 1)
            dve.tensor_tensor(kpart[:, 0, halves[0]], part[:, 0, halves[0]], part[:, 0, halves[0]], ALU.mult).then_inc(s["xsq"], 1)
            rest(ps[:, 4, :], DK ** -0.5, part[:], halves[0])
            other_parts(part[:], s["xq_parts"], halves[0])
            dve.wait_ge(s["xq_first"], 2)
            dve.tensor_tensor(kpart[:, 0, halves[1]], part[:, 0, halves[1]], part[:, 0, halves[1]], ALU.mult).then_inc(s["xsq"], 1)
            rest(ps[:, 5, :], DK ** -0.5, part[:], halves[1])
            dve.wait_ge(s["x_norm"], 1)
            step(dve.reduce_max(col[:, 4:5], ps[:, 6:8, :].rearrange("p b n -> p (b n)"), AX.X))
            dve.tensor_scalar(col[:, 1:2], col[:, 4:5], col[:, 0:1], 1.03, ALU.mult, ALU.mult).then_inc(s["bound_col"], 1)
            dve.wait_ge(s["bound_root"], 1)
            step(dve.tensor_scalar(col[:, 4:5], col[:, 3:4], -1.0 if force_exact else SAFE, None, ALU.is_gt))
            step(dve.tensor_copy(flag[:], col[0:1, 4:5]))
            step(dve.tensor_scalar(col[:, 5:6], col[:, 4:5], -1.0, 1.0, ALU.mult, ALU.add))
            step(dve.scalar_tensor_tensor(col[:, 6:7], col[:, 3:4], -1.0, col[:, 5:6], ALU.mult, ALU.mult))
            step(dve.tensor_scalar(col[:, 6:7], col[:, 6:7], -1.0, None, ALU.add))
            step(dve.tensor_scalar(col[:, 7:8], ident[:, ROWS - 1:ROWS], col[:, 6:7], 1.0, ALU.mult, ALU.add))
            dve.wait_ge(s["pool_step"], 12)
            rows = KX[SHIFT:ROWS].rearrange("r b p n -> r (b p n)")
            dve.tensor_scalar(rows, rows, col[SHIFT:ROWS, 7:8], None, ALU.mult).then_inc(s["flag_ready"], 1)
            dve.wait_ge(s["xq_parts"], 1)
            other_parts(part[:], s["xq_parts"], halves[1])
            dve.wait_ge(s["flag_ready"], 1)
            exact = dve.value_load(flag[0:1, 0:1], min_val=0, max_val=1)
            with dve.If(exact > 0):
                dve.memset(mx[:], -3.0e38).then_inc(s["slow_reduced"], 4)

                def fold(t, n):
                    with dve.Fori(0, NP) as i:
                        for sl in range(2):
                            v = t * H + i * 2
                            dve.wait_ge(s["slow_scores"], v + (sl + 1))
                            dve.wait_ge(s["slow_reduced"], (v + sl) * 2 + 4)
                            dve.tensor_reduce(mtmp[:], ps[:, 2 * sl:2 * sl + 2, :].rearrange("p b (t n) -> p (b t) n", n=P)[:, :, 0:n],
                                              AX.X, ALU.max).then_inc(s["slow_reduced"], 1)
                            dve.wait_ge(s["slow_reduced"], (v + sl) * 2 + 5)
                            m = mx[:, bass.ds(i * (2 * NT) + sl * NT, NT)]
                            dve.tensor_tensor(m, m, mtmp[:], ALU.max).then_inc(s["slow_reduced"], 1)

                with dve.Fori(0, KT - 1) as t:
                    fold(t, P)
                fold(KT - 1, TAIL)
                dve.wait_ge(s["slow_reduced"], 2 * KT * H + 4)
                dve.tensor_scalar(npart[:, 0, :], mx[:], -1.0, None, ALU.mult).then_inc(s["slow_neg"], 1)
                dve.wait_ge(s["slow_neg"], 1)
                dve.scalar_tensor_tensor(nrem[:], mx[:], -1.0, npart[:, 0, :], ALU.mult, ALU.subtract).then_inc(s["slow_neg"], 1)
                dve.wait_ge(s["slow_neg"], 2)
                dve.tensor_copy(npart[:, 1, :], nrem[:]).then_inc(s["slow_neg"], 1)
                dve.wait_ge(s["slow_neg"], 3)
                dve.tensor_tensor(npart[:, 2, :], nrem[:], npart[:, 1, :], ALU.subtract).then_inc(s["slow_neg"], 1)
                dve.wait_ge(s["slow_t"], 1)
                dve.tensor_copy(nT[:], ps[0:64, 0:2, :].bitcast(bf16)[:, :, 0:3 * P].rearrange("p h (i q) -> p h i q", i=3)).then_inc(s["slow_copied"], 1)

            def stage(step_no, src, r):
                if step_no is not None:
                    dve.wait_ge(s["x_pv"], step_no * 4 - 8)
                dve.tensor_copy(VX[:, r, :, :, 0:9], src.rearrange("p (j c) d -> p c j d", j=4)).then_inc(s["v_staged"], 1)

            for qb in range(2):
                for t in range(3):
                    stage(KT + t if qb else None, V9[:, t, :, :], t)
                with dve.Fori(1, KT // 3) as i:
                    for r in range(3):
                        stage(3 * i + (qb * KT + r), V9[:, bass.ds(3 * i + r, 1), :, :].rearrange("p o h d -> p (o h) d"), r)
                dve.wait_ge(s["x_pv"], (qb + 1) * KT * UNITS // 2)
                dve.tensor_copy(OT[:, :, qb * HALF:qb * HALF + HALF], ps[:, 6:8, :]).then_inc(s["x_out"], 1)
            finish(1)

            nred = [0]

            def absmax(src, n):
                return dve.tensor_reduce(col[:, 20 + n:21 + n], src, AX.X, ALU.max, apply_absolute_value=True)

            def to_all():
                dve.reduce_max(col[:, 8:9], col[:, 20:23], AX.X).then_inc(s["am_col"], 1)

            def scale_of(to, factor, unit=None):
                nred[0] += 1
                dve.wait_ge(s["am_all"], nred[0])
                if unit is None:
                    step(dve.tensor_scalar(col[:, to:to + 1], col[:, 9:10], 1.0 / QMAX, 1e-12, ALU.mult, ALU.max))
                    step(dve.reciprocal(col[:, factor:factor + 1], col[:, to:to + 1]))
                else:
                    step(dve.tensor_scalar(col[:, 13:14], col[:, 9:10], unit, 1.0 / QMAX, ALU.mult, ALU.mult))
                    step(dve.tensor_scalar(col[:, to:to + 1], col[:, 13:14], 1e-12, None, ALU.max))
                    step(dve.reciprocal(col[:, 13:14], col[:, to:to + 1]))
                    step(dve.tensor_scalar(col[:, factor:factor + 1], col[:, 13:14], unit, None, ALU.mult))

            def rounded(t, src, factor=11):
                return dve.tensor_scalar(t, src, col[:, factor:factor + 1], MAGIC, ALU.mult, ALU.add)

            def clipped(t):
                return dve.tensor_scalar(t, t, MAGIC + QMAX, -MAGIC, ALU.min, ALU.add)

            dve.wait_ge(ln[2]["norm"], 2)
            dve.tensor_reduce(col[:, 8:9], XN[:], AX.XY, ALU.max, apply_absolute_value=True).then_inc(s["am_col"], 1)
            scale_of(10, 11)
            for h in range(2):
                dve.wait_ge(ln[2]["T"], h + 1)
                step(rounded(XT[:, halves[h]], ps[:, h, :]))
                clipped(XT[:, halves[h]]).then_inc(ln[2]["copied"], 1)
            for t in range(3):
                dve.wait_ge(s["up_copied"], t + 1)
                step(absmax(UP[:, t, :], t))
            to_all()
            scale_of(12, 19, unit=col[:, 10:11])
            for t in range(3):
                dve.wait_ge(s["gate_copied"], t + 1)
                step(absmax(GA[:, t, :], t))
                if t < 2:
                    step(rounded(UP[:, t, :], UP[:, t, :], 19))
            to_all()
            step(clipped(UP[:, 0, :]))
            step(clipped(UP[:, 1, :]))
            scale_of(14, 11, unit=col[:, 10:11])
            marks = [mark(rounded(GA[:, t, :], GA[:, t, :])) for t in range(3)]
            for t in range(3):
                after(marks[t])
                clipped(GA[:, t, :]).then_inc(s["gate_q"], 1)
            dve.wait_ge(s["gate_q"], 3)
            step(dve.tensor_scalar(col[:, 17:18], col[:, 14:15], 1.0 / 65536.0, None, ALU.mult))
            for t in range(4):
                if t < 3:
                    dve.wait_ge(s["sig_done"], t + 1)
                    clip = mark(dve.tensor_scalar(FB[:, t, :], FB[:, t, :], MAGIC + 65535.0, -MAGIC, ALU.min, ALU.add))
                if t:
                    after(product)
                    largest = mark(absmax(GA[:, t - 1, :], t - 1))
                if t < 3:
                    after(clip)
                    product = mark(dve.scalar_tensor_tensor(GA[:, t, :], GA[:, t, :], col[:, 17:18], FB[:, t, :], ALU.mult, ALU.mult))
            after(largest)
            to_all()
            step(rounded(UP[:, 2, :], UP[:, 2, :], 19))
            step(clipped(UP[:, 2, :]))
            scale_of(15, 11)
            marks = [mark(rounded(GA[:, t, :], GA[:, t, :])) for t in range(3)]
            for t in range(3):
                after(marks[t])
                marks[t] = mark(clipped(GA[:, t, :]))
            for t in range(3):
                after(marks[t])
                marks[t] = mark(dve.tensor_tensor(GA[:, t, :], GA[:, t, :], UP[:, t, :], ALU.mult))
            for t in range(3):
                after(marks[t])
                marks[t] = mark(absmax(GA[:, t, :], t))
            after(marks[2])
            to_all()
            step(dve.tensor_scalar(col[:, 18:19], col[:, 15:16], col[:, 12:13], None, ALU.mult))
            scale_of(16, 11, unit=col[:, 18:19])
            marks = [mark(rounded(GA[:, :, at], GA[:, :, at])) for at in halves]
            for h in range(2):
                after(marks[h])
                clipped(GA[:, :, halves[h]]).then_inc(s["oq_ready"], 1)
            for half in range(2):
                dve.wait_ge(s["y_ready"], half + 1)
                xs = slice(4 * half, 4 * half + 4)
                dve.scalar_tensor_tensor(XN[:, xs, :], ps[:, 4 + half, :].rearrange("p (t d) -> p t d", t=4), col[:, 16:17],
                                         X[:, xs, :], ALU.mult, ALU.add).then_inc(s["y_done"], 1)

        @block.tensor
        def _(pe):
            mm = pe.matmul

            def norm_t(k):
                for t in range(NT):
                    if t % 4 == 0:
                        pe.wait_ge(ln[k]["norm"], t // 4 + 1)
                    last = pe.transpose(ps[:, t // 4, (t % 4) * P:(t % 4) * P + P], XN[:, t, :], ident[:])
                    if t % 4 == 3:
                        last.then_inc(ln[k]["T"], 1)

            def keep_warm(n, bank):
                nought = zeros[:].rearrange("p (o n) -> p o n", o=1).to_broadcast([P, 4, P])
                for _ in range(n):
                    mm(ps[:, bank, :].rearrange("p (t n) -> p t n", t=4), zeros[:], nought, start=True, stop=True)

            pe.wait_ge(s["consts"], 16)
            norm_t(0)
            pe.wait_ge(s["weights_loaded"], 192)
            for half in range(2):
                pe.wait_ge(ln[0]["copied"], half + 1)
                xt = XT[:, half * 512:half * 512 + 512]
                mm(ps[0:DC, 4 + half, :], w_dkv[:], xt, start=True, stop=True).then_inc(s["lat_ready"], 1)
                mm(ps[0:DC, 2 + half, :], w_dq[:], xt, start=True, stop=True).then_inc(s["lat_ready"], 1)
            pe.wait_ge(s["lat_copied"], 3)
            for half in range(2):
                last = mm(ps[:, half, :], w_uq[:], lat[:, 0, half * 512:half * 512 + 512], start=True, stop=True)
            last.then_inc(s["qk_ready"], 1)
            for half in range(2):
                last = mm(ps[:, 2 + half, :], w_uk[:], lat[:, 1, half * 512:half * 512 + 512], start=True, stop=True)
            last.then_inc(s["qk_ready"], 1)
            for t in range(NT):
                last = mm(ps[:, 6 + t // 4, (t % 4) * P:(t % 4) * P + P], lat[:, 1, t * P:t * P + P], w_uv[:], start=True, stop=True)
                if t % 4 == 3:
                    last.then_inc(s["vs_ready"], 1)

            def chunk_step(k, c, b, n, tiles):
                if k in (0, 1):
                    if k == 0:
                        pe.wait_ge(s["ctxT_ready"], c + GRANT)
                    mine = tiles[2 * k:2 * k + 2]
                    for t, m in mine:
                        last = pe.transpose(ps[:, 4, t * P:t * P + m], C[0:m, b, t, :], ident[0:m, 0:m])
                    if k == 1:
                        last.then_inc(s["ctx_t_ready"], 1)
                elif k == 2:
                    pe.wait_ge(s["ctxT_ready"], c + (1 + GRANT))
                    pe.wait_ge(s["k_sq"], c + GRANT)
                    mm(ps[:, 5, 0:n], w_k[:], CT[:, b, 0:n], start=True, stop=True).then_inc(s["k_ready"], 1)
                elif k < 7:
                    if k == 3:
                        pe.wait_ge(s["v_copied"], c + GRANT)
                    if k - 3 < len(tiles):
                        t, m = tiles[k - 3]
                        last = mm(ps[0:m, 6, t * P:t * P + P], CT[:, b, t * P:t * P + m], w_v[:], start=True, stop=True)
                        if t == len(tiles) - 1:
                            last.then_inc(s["v_ready"], 1)
                else:
                    pe.wait_ge(s["k_sq"], c + (1 + GRANT))
                    pe.wait_ge(s["n_copied"], c + GRANT)
                    mm(ps[:, 7, 0:n], headsum[:], csq[:, 0:n], start=True, stop=True).then_inc(s["n_ready"], 1)

            def max_block(i, v):
                slot, qt, high, n = max_blocks()[v]
                pe.wait_ge(s["m_reduced"], i * BLOCKS + (v + 1))
                if isinstance(i, int):
                    lhs, rhs = QQ[0:SELF_ROWS, 2 * i + slot, qt * P:qt * P + P], KS[0:SELF_ROWS, i, :]
                else:
                    lhs = QQ[0:SELF_ROWS, bass.ds(i * 2 + slot, 1), qt * P:qt * P + P].rearrange("r o q -> r (o q)")
                    rhs = KS[0:SELF_ROWS, bass.ds(i, 1), :].rearrange("r o k -> r (o k)")
                diag = high or qt < 4
                last = mm(ps[:, v % 4, 0:n], lhs, rhs[:, HALF * high:HALF * high + n], start=True, stop=not diag)
                if diag:
                    last = mm(ps[:, v % 4, n - P:n], identb[:], mask[:, 1, :], start=False, stop=True)
                last.then_inc(s["m_scores"], 1)

            def negs(banks, done):
                for hh, bank in banks:
                    for k in range(3):
                        last = pe.transpose(ps[0:64, bank, :].bitcast(bf16)[:, k * P:k * P + P], npart[:, k, 64 * hh:64 * hh + 64], identb[:])
                last.then_inc(done, 1)

            pe.wait_ge(s["pool_init"], 1)
            pe.wait_ge(s["ks_stored"], 16)
            keep_warm(20, 4)
            pe.wait_ge(q_spread[0], 192)
            pe.wait_ge(ks_spread[0], KLOAD)
            pe.wait_ge(s["vs_copied"], NT)
            pe.wait_ge(s["identb_ready"], 1)
            whole = [(t, P) for t in range(CH)]
            AT = (0, 1, 5, 7, 8, 9, 10, 11)

            def pair(i):
                for v in range(BLOCKS):
                    max_block(i, v)
                    slot = v // (BLOCKS // 2)
                    if v % (BLOCKS // 2) in AT:
                        k = AT.index(v % (BLOCKS // 2))
                        if k == 0:
                            pe.wait_ge(ctx_loaded[slot], 16 * i + 16)
                        chunk_step(k, 2 * i + slot, slot, CH * P, whole)

            with pe.Fori(0, NP // 2) as i:
                pair(i)
            pe.wait_ge(s["neg_parts"], 1)
            negs([(0, 0)], s["neg_t"])
            pe.wait_ge(s["neg_copied"], 1)
            pe.wait_ge(q_spread[1], 192)
            pe.wait_ge(ks_spread[1], KLOAD)
            with pe.Fori(NP // 2, NCH // 2) as i:
                pair(i)
            pe.wait_ge(s["ctx_tail_loaded"], 32)
            for v in range(BLOCKS):
                max_block(NCH // 2, v)
                if v in AT:
                    chunk_step(AT.index(v), NCH, 0, REST, [(0, P), (1, P), (2, TAIL)])
                if v == BLOCKS // 2:
                    pe.wait_ge(s["w_ready"], 1)
                    pe.wait_ge(s["v_copied"], NCH + 1 + GRANT)
                if BLOCKS // 2 <= v < BLOCKS // 2 + 9:
                    w = v - BLOCKS // 2
                    last = pe.transpose(ps[:, 4 + w // 3, (w % 3) * P:(w % 3) * P + P], wraw[:, w, :], ident[:])
                    if w % 3 == 2:
                        last.then_inc(s["w_t_ready"], 1)

            def self_scores(u, hh, qb, kt, p):
                if u:
                    pe.wait_ge(s["self_exp"], u if u <= EARLY else max(EARLY, u - 2))
                if (hh, qb, kt, p) == (1, 0, 0, 4):
                    pe.wait_ge(s["neg_rows"], 96)
                lo = first_query(qb, kt)
                diag = kt >= 4 * qb
                for a in range(2):
                    bank = ps[:, self_bank(u) + a, :]
                    last = mm(bank[:, lo:HALF], KS[0:SELF_ROWS, p, kt * P:kt * P + P], QQ[0:SELF_ROWS, 2 * p + a, qb * HALF + lo:qb * HALF + HALF],
                              start=True, stop=not diag)
                    if diag:
                        last = mm(bank[:, lo:lo + P], identb[:], mask[:, 0, :], start=False, stop=True)
                last.then_inc(s["self_ready"], 1)

            def window(v, h):
                c, j = h % 4, h // 4
                lo = 32 * j - 9 * (j % 2)
                return v[:, c].rearrange("p j e -> p (j e)")[:, lo:lo + 32]

            def four_heads(v, pair, lo, start=False, stop=False, at=None, bank=None):
                at = pair if at is None else at
                place = pair // 2
                odd = place % 2
                bank = 6 + place // 2 if bank is None else bank
                for h in range(2 * pair, 2 * pair + 4):
                    c = h % 4
                    last = mm(ps[32 * c:32 * c + 32, bank, lo:HALF], window(v, h), PR[:, at + h // 2 - pair, h % 2, lo:HALF],
                              start=start and not odd, stop=bool(stop and odd))
                return last

            units = self_units()
            LAG = 2
            groups = len(units) // 2

            def products(g):
                if g == EARLY // 2 + 1:
                    pe.wait_ge(s["neg_parts"], 2)
                    negs([(1, 7)], s["neg_t"])
                if g >= LAG:
                    hh, qb, kt, p = units[2 * (g - LAG)]
                    if hh == 1 and (kt, p) == (0, 4):
                        pe.wait_ge(s["self_out"], qb + 1)
                    if (hh, qb, kt, p) == (0, 1, 0, 0):
                        pe.wait_ge(s["neg_copied"], 2)
                    pe.wait_ge(s["self_exp"], 2 * (g - LAG) + 2)
                    four_heads(VS[:, kt], p, first_query(qb, kt), kt == 0, kt == 4 * qb + 3, at=2 * (g - LAG) % 8, bank=6 + qb).then_inc(s["self_pv"], 1)

            for v in range(BLOCKS):
                max_block(NCH // 2 + 1, v)
                if v == 1:
                    pe.wait_ge(s["w_t_copied"], 3)
                    pe.wait_ge(s["n_copied"], NCH + 1 + GRANT)
                    pe.wait_ge(s["neg_rows"], 48)
                if v % 3 == 2:
                    self_scores(v // 3, *units[v // 3])
                    if v % 6 == 5:
                        products(v // 6)
            pe.wait_ge(s["m_reduced"], BLOCKS * NP + 4)
            for g in range(EARLY // 2, groups + LAG):
                if g < groups:
                    for u in (2 * g, 2 * g + 1):
                        self_scores(u, *units[u])
                products(g)

            def finish(k, out_ready, before, w):
                for h in range(2):
                    pe.wait_ge(out_ready, before + h + 1)
                    for a in range(2):
                        for t in range(4):
                            last = pe.transpose(ps[:, 2 * h + a, t * P:t * P + P], OT[:, a, (4 * h + t) * P:(4 * h + t) * P + P], ident[:])
                    last.then_inc(fin[k]["back"], 1)
                for h in range(2):
                    pe.wait_ge(fin[k]["attn"], h + 1)
                    for t in range(4):
                        last = pe.transpose(ps[:, 2 * h, t * P:t * P + P], XN[:, 4 * h + t, :], ident[:])
                    last.then_inc(fin[k]["attnT"], 1)
                for h in range(2):
                    pe.wait_ge(fin[k]["attnTc"], h + 1)
                    for t in range(4):
                        last = mm(ps[:, 2 * h + 1, t * P:t * P + P], XT[:, (4 * h + t) * P:(4 * h + t) * P + P], w[:], start=True, stop=True)
                    last.then_inc(fin[k]["y"], 1)

            finish(0, s["self_out"], 2, w_os)
            norm_t(1)
            for half in range(2):
                pe.wait_ge(ln[1]["copied"], half + 1)
                mm(ps[:, 4 + half, :], w_q[:], XT[:, half * 512:half * 512 + 512], start=True, stop=True).then_inc(s["xq_ready"], 1)
            for half in range(2):
                pe.wait_ge(s["xsq"], half + 1)
                last = mm(ps[:, 6 + half, :], headsum[:], kpart[:, 0, half * 512:half * 512 + 512], start=True, stop=True)
            last.then_inc(s["x_norm"], 1)
            pe.wait_ge(s["flag_ready"], 1)
            keep_warm(20, 6)
            pe.wait_ge(s["q_cleared"], 1)
            pe.wait_ge(kx_loaded[0], KLOAD)
            pe.wait_ge(xq_spread[0], 192)
            exact = pe.value_load(flag[0:1, 0:1], min_val=0, max_val=1)
            with pe.If(exact > 0):
                pe.wait_ge(xq_spread[1], 192)

                def scan(t, n, loaded):
                    with pe.Fori(0, NP) as i:
                        if loaded is not None:
                            pe.wait_ge(s["slow_loaded"], loaded)
                        for sl in range(2):
                            v = t * H + i * 2
                            pe.wait_ge(s["slow_reduced"], (v + sl) * 2 + 1)
                            for qt in range(NT):
                                last = mm(ps[:, 2 * sl + qt // 4, (qt % 4) * P:(qt % 4) * P + n],
                                          QQ[0:ROWS, bass.ds(i * 2 + sl, 1), qt * P:qt * P + P].rearrange("r o q -> r (o q)"),
                                          KX[:, 0, bass.ds(i, 1), 0:n].rearrange("r o k -> r (o k)"), start=True, stop=True)
                            last.then_inc(s["slow_scores"], 1)

                scan(0, P, None)
                with pe.Fori(1, KT - 1) as t:
                    scan(t, P, t * KLOAD)
                scan(KT - 1, TAIL, (KT - 1) * KLOAD)
                pe.wait_ge(s["slow_neg"], 4)
                negs([(0, 0), (1, 1)], s["slow_t"])
                pe.wait_ge(s["slow_loaded"], KT * KLOAD)
                pe.wait_ge(s["slow_rows"], 96)

            def clear():
                for bank in (6, 7):
                    mm(ps[:, bank, :], zeros[0:ROWS, :], QQ[0:ROWS, 0, 0:HALF], start=True, stop=False)

            def close():
                for bank in (6, 7):
                    last = mm(ps[:, bank, :], zeros[0:ROWS, :], QQ[0:ROWS, 0, 0:HALF], start=False, stop=True)
                return last

            def cross_tile(qb, units_before, tiles_before, r, loaded, first=False):
                pe.wait_ge(kx_loaded[r], loaded)
                if first and qb:
                    pe.wait_ge(xq_spread[1], 192)
                for p in range(UNITS):
                    if not (first and qb == 0 and p < 3):
                        pe.wait_ge(s["x_exp"], units_before + (p - 2))
                    b = 2 * ((UNITS * r + p) % 3)
                    for a in range(2):
                        last = mm(ps[:, b + a, :], KX[:, r, p, :], QQ[0:ROWS, 2 * p + a, qb * HALF:qb * HALF + HALF],
                                  start=True, stop=True)
                    last.then_inc(s["xs_ready"], 1)
                    if p % 2 == 0 or (first and qb == 0 and p < 5):
                        continue
                    if p == 5:
                        pe.wait_ge(s["v_staged"], tiles_before + 1)
                        if first:
                            if qb:
                                pe.wait_ge(s["x_out"], 1)
                            clear()
                    pe.wait_ge(s["x_exp"], units_before + (p - 3))
                    last = four_heads(VX[:, r if p > 3 else (r - 1) % 3], (p - 5) % UNITS, 0)
                    if first and p == 3:
                        last = close()
                    last.then_inc(s["x_pv"], 1)

            for qb in range(2):
                for r in range(3):
                    t = qb * KT + r
                    cross_tile(qb, UNITS * t, t, r, KLOAD * (KT // 3 * qb + 1), first=r == 0)
                with pe.Fori(1, KT // 3) as i:
                    for r in range(3):
                        cross_tile(qb, i * (3 * UNITS) + UNITS * (qb * KT + r), i * 3 + (qb * KT + r), r,
                                   i * KLOAD + KLOAD * (KT // 3 * qb + 1))
            pe.wait_ge(s["x_exp"], 2 * KT * UNITS)
            four_heads(VX[:, (KT - 1) % 3], UNITS - 4, 0).then_inc(s["x_pv"], 1)
            four_heads(VX[:, (KT - 1) % 3], UNITS - 2, 0)
            close().then_inc(s["x_pv"], 1)
            finish(1, s["x_out"], 0, w_ox)

            norm_t(2)
            keep_warm(8, 7)
            pe.wait_ge(ln[2]["copied"], 2)
            for t in range(3):
                for g in range(2):
                    last = mm(ps[:, 2 * t + g, :], wT[:, 3 + t, :], XT[:, 512 * g:512 * g + 512], start=True, stop=True)
                last.then_inc(s["up_ready"], 1)
            for t in range(3):
                if t:
                    pe.wait_ge(s["up_copied"], t)
                for g in range(2):
                    last = mm(ps[:, 2 * ((t + 3) % 4) + g, :], wT[:, t, :], XT[:, 512 * g:512 * g + 512], start=True, stop=True)
                last.then_inc(s["gate_ready"], 1)
            pe.wait_ge(s["am_col"], 5)
            keep_warm(14, 7)
            for t in range(NT):
                if t % 4 == 0:
                    pe.wait_ge(s["oq_ready"], t // 4 + 1)
                for k in range(3):
                    last = mm(ps[:, 4 + t // 4, (t % 4) * P:(t % 4) * P + P], GA[:, k, t * P:t * P + P], wT[:, 6 + k, :],
                              start=k == 0, stop=k == 2)
                if t % 4 == 3:
                    last.then_inc(s["y_ready"], 1)


_INS = ['x', 'ctx_1024', 'L0_attn_W_dq', 'L0_attn_W_uq', 'L0_attn_W_dkv', 'L0_attn_W_uk', 'L0_attn_W_uv', 'L0_attn_W_o',
        'L0_xattn_Wq', 'L0_xattn_Wk', 'L0_xattn_Wv', 'L0_xattn_Wo', 'L0_ffn_w_gate', 'L0_ffn_w_up', 'L0_ffn_w_down']

_BY_DIM = ('L0_attn_W_uq', 'L0_attn_W_uk', 'L0_xattn_Wq', 'L0_xattn_Wk')


def kernel(**inputs):
    import ml_dtypes
    import concourse.bacc as _bacc
    from concourse.bass_utils import run_bass_kernel_spmd as _run

    nc = _bacc.Bacc("TRN2", target_bir_lowering=False, num_devices=1)
    at = np.arange(P)
    masks = np.zeros((P, 2, P), np.float32)
    masks[:, 0, :] = np.where(at[:, None] > at[None, :], MASKED, 0.0)
    masks[:, 1, :] = np.where(at[None, :] > at[:, None], MASKED, 0.0)
    heads = (at[:, None] % NP == at[None, :] % NP) & (at[:, None] // (NP * DK) == at[None, :] // (NP * DK))
    arrays, args = {}, []
    for name in _INS:
        a = inputs[name]
        if name in _BY_DIM:
            a = np.asarray(a).reshape(-1, NP, 2 * DK).transpose(0, 2, 1).reshape(-1, D)
        a = np.ascontiguousarray(a)
        arrays[f"in_{name}"] = a
        args.append(nc.dram_tensor(f"in_{name}", a.shape, mybir.dt.from_np(a.dtype), kind="ExternalInput").ap())
    for name, a in (("ident", np.eye(P, dtype=np.float32)), ("masks", masks.astype(ml_dtypes.bfloat16)),
                    ("heads", heads.astype(ml_dtypes.bfloat16))):
        arrays[f"const_{name}"] = a
        args.append(nc.dram_tensor(f"const_{name}", a.shape, mybir.dt.from_np(a.dtype), kind="ExternalInput").ap())
    args.append(nc.dram_tensor("out", (1, S, D), mybir.dt.float32, kind="ExternalOutput").ap())
    build(nc, *args)
    r = _run(nc, [arrays], core_ids=[0])
    return r.results[0]["out"]
```
